# Optimizing a Trainium2 kernel written in Bass

```python
import numpy as np
import jax
import jax.numpy as jnp

def _softmax(x, axis=-1):
    return jax.nn.softmax(x, axis=axis)

def _gelu(x):
    return jax.nn.gelu(x, approximate=True)

def _silu(x):
    return jax.nn.silu(x)

def _sigmoid(x):
    return jax.nn.sigmoid(x)

def _layernorm(x, axis=-1, eps=1e-05):
    m = jnp.mean(x, axis=axis, keepdims=True)
    v = jnp.var(x, axis=axis, keepdims=True)
    return (x - m) / jnp.sqrt(v + eps)

def _scatter_add(tgt, idx, src, axis=0):
    return tgt.at[idx].add(src)

def _segment_sum(src, seg, n):
    return jax.ops.segment_sum(src, seg, n)
kernel_name = 'mk_cond_seq_d2_seqx_r4_0108dc'

def setup_inputs(seed: int=0):
    np.random.seed(seed)
    _w = jnp.asarray

    def _rec_inputs():
        import jax
        import jax.numpy as jnp
        _rk = jax.random.key(seed)
        x = -0.0002928 + 1 * jax.random.normal(jax.random.fold_in(_rk, 1), (8, 256, 256), jnp.float32)
        _lenS = 256 - jax.random.randint(jax.random.fold_in(_rk, 7), (8,), 0, max(1, 256 // 4) + 1, jnp.int32)
        _lenS2 = 256 - jax.random.randint(jax.random.fold_in(_rk, 8), (8,), 0, max(1, 256 // 4) + 1, jnp.int32)
        itok_B_6_14 = jax.random.randint(jax.random.fold_in(_rk, 11), (8,), 6, 15, jnp.int32)
        condB_dt = jax.random.uniform(jax.random.fold_in(_rk, 12), (8,), jnp.float32, 0.0, 0.981965)
        return (x, itok_B_6_14, condB_dt)
    x, itok_B_6_14, condB_dt = _rec_inputs()

    def _L0_cond_setup():
        import jax, jax.numpy as jnp
        import numpy as np
        D = 256
        E = 8
        FF = 1024
        TOPK = 2
        S = 32
        SE = 64
        SH = 128
        B, T = (2, 512)

        def _forward(x, subject_ids, ln_g, ln_b, subj_emb, hyp_w1, hyp_b1, hyp_w2, hyp_b2, sty_w1, sty_b1, sty_w2, sty_b2, router_w, exp_w1, exp_b1, exp_w2, exp_b2):
            mu = x.mean(-1, keepdims=True)
            var = x.var(-1, keepdims=True)
            h = (x - mu) * jax.lax.rsqrt(var + 1e-05) * ln_g + ln_b
            m_t = h.mean(1, keepdims=True)
            v_t = h.var(1, keepdims=True)
            h_norm = (h - m_t) * jax.lax.rsqrt(v_t + 1e-08)
            se = subj_emb[subject_ids]
            hyp = jax.nn.relu(se @ hyp_w1 + hyp_b1) @ hyp_w2 + hyp_b2
            sty = jax.nn.relu(hyp @ sty_w1 + sty_b1) @ sty_w2 + sty_b2
            gamma, beta = jnp.split(sty, 2, axis=-1)
            gamma = jax.nn.softplus(gamma) + 1e-08
            h = h_norm * gamma[:, None, :] + beta[:, None, :]
            h_flat = h.reshape(-1, D)
            probs = jax.nn.softmax(h_flat @ router_w, axis=-1)
            gates, idx = jax.lax.top_k(probs, TOPK)
            gates = gates / gates.sum(-1, keepdims=True)
            N = h_flat.shape[0]
            combine = jnp.zeros((N, E), h_flat.dtype).at[jnp.arange(N)[:, None], idx].add(gates)
            hid = jax.nn.relu(jnp.einsum('nd,edf->nef', h_flat, exp_w1) + exp_b1)
            eout = jnp.einsum('nef,efd->ned', hid, exp_w2) + exp_b2
            y = jnp.einsum('ned,ne->nd', eout, combine)
            return x + y.reshape(x.shape)
        key = jax.random.key(seed)
        ks = jax.random.split(key, 16)
        n = lambda k, sh, s=0.02: jax.random.normal(k, sh, dtype=jnp.float32) * s
        return {'x': jax.random.normal(ks[0], (B, T, D), dtype=jnp.float32), 'subject_ids': jax.random.randint(ks[1], (B,), 0, S), 'ln_g': jnp.ones((D,), jnp.float32), 'ln_b': jnp.zeros((D,), jnp.float32), 'subj_emb': n(ks[2], (S, SE)), 'hyp_w1': n(ks[3], (SE, SH), 1.0 / np.sqrt(SE)), 'hyp_b1': jnp.zeros((SH,), jnp.float32), 'hyp_w2': n(ks[4], (SH, SH), 1.0 / np.sqrt(SH)), 'hyp_b2': jnp.zeros((SH,), jnp.float32), 'sty_w1': n(ks[5], (SH, SH // 2), 1.0 / np.sqrt(SH)), 'sty_b1': jnp.zeros((SH // 2,), jnp.float32), 'sty_w2': n(ks[6], (SH // 2, 2 * D), 1.0 / np.sqrt(SH // 2)), 'sty_b2': jnp.zeros((2 * D,), jnp.float32), 'router_w': n(ks[7], (D, E), 1.0 / np.sqrt(D)), 'exp_w1': n(ks[8], (E, D, FF), 1.0 / np.sqrt(D)), 'exp_b1': jnp.zeros((E, FF), jnp.float32), 'exp_w2': n(ks[9], (E, FF, D), 1.0 / np.sqrt(FF)), 'exp_b2': jnp.zeros((E, D), jnp.float32)}
    _L0_cond_all = _L0_cond_setup()
    _L0_cond_in = {k: v for k, v in _L0_cond_all.items() if k in ('ln_g', 'ln_b', 'subj_emb', 'hyp_w1', 'hyp_b1', 'hyp_w2', 'hyp_b2', 'sty_w1', 'sty_b1', 'sty_w2', 'sty_b2', 'router_w', 'exp_w1', 'exp_b1', 'exp_w2', 'exp_b2')}
    del _L0_cond_all

    def _L1_cond_setup():
        import jax, jax.numpy as jnp
        import numpy as np
        B, NX, NY = (16, 256, 256)

        def _grad(f, axis):
            fm = jnp.moveaxis(f, axis, -1)
            g = (jnp.roll(fm, -1, -1) - jnp.roll(fm, 1, -1)) * 0.5
            g0 = (-3.0 * fm[..., 0] + 4.0 * fm[..., 1] - fm[..., 2]) * 0.5
            gN = (3.0 * fm[..., -1] - 4.0 * fm[..., -2] + fm[..., -3]) * 0.5
            g = g.at[..., 0].set(g0).at[..., -1].set(gN)
            return jnp.moveaxis(g, -1, axis)

        def _grad2(f, axis):
            fm = jnp.moveaxis(f, axis, -1)
            g = jnp.roll(fm, -1, -1) - 2.0 * fm + jnp.roll(fm, 1, -1)
            g0 = 2.0 * fm[..., 0] - 5.0 * fm[..., 1] + 4.0 * fm[..., 2] - fm[..., 3]
            gN = 2.0 * fm[..., -1] - 5.0 * fm[..., -2] + 4.0 * fm[..., -3] - fm[..., -4]
            g = g.at[..., 0].set(g0).at[..., -1].set(gN)
            return jnp.moveaxis(g, -1, axis)
        key = jax.random.key(seed)
        k1, k2, k3, k4 = jax.random.split(key, 4)
        f = jax.random.uniform(k1, (B, NX, NY), dtype=jnp.float32)
        A_grid = jax.random.normal(k2, (2, NX, NY), dtype=jnp.float32)
        B_grid = jax.random.uniform(k3, (3, NX, NY), dtype=jnp.float32)
        dt = jax.random.uniform(k4, (B,), dtype=jnp.float32)
        return {'f': f, 'A_grid': A_grid, 'B_grid': B_grid, 'dt': dt}
    _L1_cond_all = _L1_cond_setup()
    _L1_cond_in = {k: v for k, v in _L1_cond_all.items() if k in ('A_grid', 'B_grid')}
    del _L1_cond_all
    return {'x': x, 'itok_B_6_14': itok_B_6_14, 'condB_dt': condB_dt, 'L0_cond_ln_g': _L0_cond_in['ln_g'], 'L0_cond_ln_b': _L0_cond_in['ln_b'], 'L0_cond_subj_emb': _L0_cond_in['subj_emb'], 'L0_cond_hyp_w1': _L0_cond_in['hyp_w1'], 'L0_cond_hyp_b1': _L0_cond_in['hyp_b1'], 'L0_cond_hyp_w2': _L0_cond_in['hyp_w2'], 'L0_cond_hyp_b2': _L0_cond_in['hyp_b2'], 'L0_cond_sty_w1': _L0_cond_in['sty_w1'], 'L0_cond_sty_b1': _L0_cond_in['sty_b1'], 'L0_cond_sty_w2': _L0_cond_in['sty_w2'], 'L0_cond_sty_b2': _L0_cond_in['sty_b2'], 'L0_cond_router_w': _L0_cond_in['router_w'], 'L0_cond_exp_w1': _L0_cond_in['exp_w1'], 'L0_cond_exp_b1': _L0_cond_in['exp_b1'], 'L0_cond_exp_w2': _L0_cond_in['exp_w2'], 'L0_cond_exp_b2': _L0_cond_in['exp_b2'], 'L1_cond_A_grid': _L1_cond_in['A_grid'], 'L1_cond_B_grid': _L1_cond_in['B_grid']}

def reference(x, itok_B_6_14, condB_dt, L0_cond_ln_g, L0_cond_ln_b, L0_cond_subj_emb, L0_cond_hyp_w1, L0_cond_hyp_b1, L0_cond_hyp_w2, L0_cond_hyp_b2, L0_cond_sty_w1, L0_cond_sty_b1, L0_cond_sty_w2, L0_cond_sty_b2, L0_cond_router_w, L0_cond_exp_w1, L0_cond_exp_b1, L0_cond_exp_w2, L0_cond_exp_b2, L1_cond_A_grid, L1_cond_B_grid):
    import jax
    import jax.numpy as jnp

    def _L0_cond_ref(x, subject_ids, ln_g, ln_b, subj_emb, hyp_w1, hyp_b1, hyp_w2, hyp_b2, sty_w1, sty_b1, sty_w2, sty_b2, router_w, exp_w1, exp_b1, exp_w2, exp_b2):
        import jax, jax.numpy as jnp
        import numpy as np
        D = 256
        E = 8
        FF = 1024
        TOPK = 2
        S = 32
        SE = 64
        SH = 128
        B, T = (2, 512)

        def _forward(x, subject_ids, ln_g, ln_b, subj_emb, hyp_w1, hyp_b1, hyp_w2, hyp_b2, sty_w1, sty_b1, sty_w2, sty_b2, router_w, exp_w1, exp_b1, exp_w2, exp_b2):
            mu = x.mean(-1, keepdims=True)
            var = x.var(-1, keepdims=True)
            h = (x - mu) * jax.lax.rsqrt(var + 1e-05) * ln_g + ln_b
            m_t = h.mean(1, keepdims=True)
            v_t = h.var(1, keepdims=True)
            h_norm = (h - m_t) * jax.lax.rsqrt(v_t + 1e-08)
            se = subj_emb[subject_ids]
            hyp = jax.nn.relu(se @ hyp_w1 + hyp_b1) @ hyp_w2 + hyp_b2
            sty = jax.nn.relu(hyp @ sty_w1 + sty_b1) @ sty_w2 + sty_b2
            gamma, beta = jnp.split(sty, 2, axis=-1)
            gamma = jax.nn.softplus(gamma) + 1e-08
            h = h_norm * gamma[:, None, :] + beta[:, None, :]
            h_flat = h.reshape(-1, D)
            probs = jax.nn.softmax(h_flat @ router_w, axis=-1)
            gates, idx = jax.lax.top_k(probs, TOPK)
            gates = gates / gates.sum(-1, keepdims=True)
            N = h_flat.shape[0]
            combine = jnp.zeros((N, E), h_flat.dtype).at[jnp.arange(N)[:, None], idx].add(gates)
            hid = jax.nn.relu(jnp.einsum('nd,edf->nef', h_flat, exp_w1) + exp_b1)
            eout = jnp.einsum('nef,efd->ned', hid, exp_w2) + exp_b2
            y = jnp.einsum('ned,ne->nd', eout, combine)
            return x + y.reshape(x.shape)
        return _forward(x, subject_ids, ln_g, ln_b, subj_emb, hyp_w1, hyp_b1, hyp_w2, hyp_b2, sty_w1, sty_b1, sty_w2, sty_b2, router_w, exp_w1, exp_b1, exp_w2, exp_b2)

    def _L1_cond_ref(f, A_grid, B_grid, dt):
        import jax, jax.numpy as jnp
        import numpy as np
        B, NX, NY = (16, 256, 256)

        def _grad(f, axis):
            fm = jnp.moveaxis(f, axis, -1)
            g = (jnp.roll(fm, -1, -1) - jnp.roll(fm, 1, -1)) * 0.5
            g0 = (-3.0 * fm[..., 0] + 4.0 * fm[..., 1] - fm[..., 2]) * 0.5
            gN = (3.0 * fm[..., -1] - 4.0 * fm[..., -2] + fm[..., -3]) * 0.5
            g = g.at[..., 0].set(g0).at[..., -1].set(gN)
            return jnp.moveaxis(g, -1, axis)

        def _grad2(f, axis):
            fm = jnp.moveaxis(f, axis, -1)
            g = jnp.roll(fm, -1, -1) - 2.0 * fm + jnp.roll(fm, 1, -1)
            g0 = 2.0 * fm[..., 0] - 5.0 * fm[..., 1] + 4.0 * fm[..., 2] - fm[..., 3]
            gN = 2.0 * fm[..., -1] - 5.0 * fm[..., -2] + 4.0 * fm[..., -3] - fm[..., -4]
            g = g.at[..., 0].set(g0).at[..., -1].set(gN)
            return jnp.moveaxis(g, -1, axis)
        Af = A_grid[None] * f[:, None]
        Bf = B_grid[None] * f[:, None]
        gradv_Af = _grad(Af[:, 0], 1) + _grad(Af[:, 1], 2)
        gradvv_Bf = _grad2(Bf[:, 0], 1) + _grad2(Bf[:, 1], 2) + _grad(_grad(Bf[:, 2], 2), 1) + _grad(_grad(Bf[:, 2], 1), 2)
        df = -gradv_Af + gradvv_Bf * 0.5
        f_new = f + df * dt[:, None, None]
        return jnp.maximum(f_new, 0.0)
    x = _L0_cond_ref(x, itok_B_6_14, L0_cond_ln_g, L0_cond_ln_b, L0_cond_subj_emb, L0_cond_hyp_w1, L0_cond_hyp_b1, L0_cond_hyp_w2, L0_cond_hyp_b2, L0_cond_sty_w1, L0_cond_sty_b1, L0_cond_sty_w2, L0_cond_sty_b2, L0_cond_router_w, L0_cond_exp_w1, L0_cond_exp_b1, L0_cond_exp_w2, L0_cond_exp_b2)
    x = _L1_cond_ref(x, L1_cond_A_grid, L1_cond_B_grid, condB_dt)
    return x

_drawn_inputs = setup_inputs


def setup_inputs(seed=0):
    import zlib

    import numpy as np

    out = dict(_drawn_inputs(seed))
    spreads = {'L0_cond_ln_g': (1.0, 0.2),
     'L0_cond_ln_b': (0.0, 0.1),
     'L0_cond_hyp_b1': (0.0, 0.1),
     'L0_cond_hyp_b2': (0.0, 0.1),
     'L0_cond_sty_b1': (0.0, 0.1),
     'L0_cond_sty_b2': (0.0, 0.1),
     'L0_cond_exp_b1': (0.0, 0.1),
     'L0_cond_exp_b2': (0.0, 0.1)}
    factors = {}
    for name, (base, spread) in spreads.items():
        noise = np.random.default_rng([zlib.crc32(name.encode()), seed]).standard_normal(out[name].shape)
        drawn = base * np.exp(spread * noise) if base else spread * noise
        out[name] = jnp.asarray(drawn.astype(out[name].dtype))
    for name, factor in factors.items():
        out[name] = (out[name] * factor).astype(out[name].dtype)
    return out
```

```python
from contextlib import ExitStack

import numpy as np

import concourse.bass as bass
from concourse import mybir

ALU = mybir.AluOpType
ACT = mybir.ActivationFunctionType
F32 = mybir.dt.float32
F32R = mybir.dt.float32r
BF16 = mybir.dt.bfloat16
I32 = mybir.dt.int32
AX_X = mybir.AxisListType.X

P = 128
NB, T, D = 8, 256, 256
N = NB * T
NJ = N // P
KD = D // P
E, FF, TOPK = 8, 1024, 2
S_SUB, SE, SH = 32, 64, 128
FB = FF // P
ST = 256
TB = ST // P
NS = N * TOPK // ST + E - 1
NC = NS * TB
BANKS = FB // 2
EMPTY = 8192.0

C_IDENT = 0
C_BEFORE = C_IDENT + P
C_EXPERT = C_BEFORE + P
C_SLOT = C_EXPERT + NJ * E
C_COL = C_SLOT + NS * E
C_ROW = C_COL + NC
C_JC = C_ROW + P
C_PART = C_JC + TOPK * NJ
C_D1 = C_PART + 2
C_D2 = C_D1 + KD * T
C_EDGE = C_D2 + KD * T
C_ALL = C_EDGE + 32


def stencil(n):
    d1, d2 = np.zeros((n, n)), np.zeros((n, n))
    for i in range(1, n - 1):
        d1[i, i - 1], d1[i, i + 1] = -0.5, 0.5
        d2[i, i - 1], d2[i, i], d2[i, i + 1] = 1, -2, 1
    d1[0, :3] = [-1.5, 2, -0.5]
    d1[-1, -3:] = [0.5, -2, 1.5]
    d2[0, :4] = [2, -5, 4, -1]
    d2[-1, -4:] = [-1, 4, -5, 2]
    return d1, d2


def constants():
    c = np.zeros((P, C_ALL), np.float32)
    p = np.arange(P)
    c[:, C_IDENT:C_IDENT + P] = np.eye(P)
    c[:, C_BEFORE:C_BEFORE + P] = p[:, None] < p[None, :]
    c[:, C_EXPERT:C_EXPERT + NJ * E] = np.tile(np.arange(E), NJ)
    c[:, C_SLOT:C_SLOT + NS * E] = np.repeat(np.arange(NS), E)
    c[:, C_COL:C_COL + NC] = np.arange(NC)
    c[:, C_ROW:C_ROW + P] = p
    c[:, C_JC:C_JC + TOPK * NJ] = np.arange(TOPK * NJ)
    c[:, C_PART] = p
    c[:, C_PART + 1] = p + 1
    d1, d2 = stencil(T)
    c[:, C_D1:C_D1 + KD * T] = d1.T.reshape(KD, P, T).transpose(1, 0, 2).reshape(P, -1)
    c[:, C_D2:C_D2 + KD * T] = 0.5 * d2.T.reshape(KD, P, T).transpose(1, 0, 2).reshape(P, -1)
    for n, (m, w) in enumerate(((d2, 0.5), (d1, -1.0), (d1, 1.0))):
        c[:, C_EDGE + 8 * n:C_EDGE + 8 * n + 4] = w * m[0, :4]
        c[:, C_EDGE + 8 * n + 4:C_EDGE + 8 * n + 8] = w * m[-1, -4:]
    return c


SMALL = {}
for _name, _rows, _cols in (("ln_g", P, KD), ("ln_b", P, KD), ("router_w", P, KD * E), ("hyp_b1", SH, 1),
                            ("hyp_b2", SH, 1), ("sty_b1", SH // 2, 1), ("sty_b2", P, 2 * D // P),
                            ("subj_emb", S_SUB, SE), ("hyp_w1", SE, SH), ("hyp_w2", SH, SH),
                            ("sty_w1", SH, SH // 2), ("sty_w2", SH // 2, 2 * D)):
    SMALL[_name] = (_rows, _cols, sum(v[1] for v in SMALL.values()))
SMALL_ALL = sum(v[1] for v in SMALL.values())


def pack(inputs):
    out = np.zeros((P, SMALL_ALL), np.float32)
    for name, (rows, cols, at) in SMALL.items():
        a = np.asarray(inputs["L0_cond_" + name])
        if name == "router_w":
            a = a.reshape(KD, P, E).transpose(1, 0, 2)
        elif a.ndim == 1 and cols > 1:
            a = a.reshape(cols, P).T
        out[:rows, at:at + cols] = a.reshape(rows, cols)
    return out


def moe_then_stencil(nc, x, ids, dt, exp_w1, exp_b1, exp_w2, exp_b2, a_grid, b_grid, small, consts, out):
    h_rows = nc.dram_tensor("h_rows", (N, D), F32, kind="Internal").ap()
    y_rows = nc.dram_tensor("y_rows", (TOPK * N, D), F32, kind="Internal").ap()

    ctx = ExitStack()
    with ctx:
        def sb(name, shape, dt_=F32):
            return ctx.enter_context(nc.sbuf_tensor(name, shape, dt_))

        def sem(name):
            return ctx.enter_context(nc.semaphore(name))

        banks = [ctx.enter_context(nc.psum_tensor(f"bank{i}", [P, 512], F32)) for i in range(8)]

        x_sb = sb("x_sb", [P, NJ, D])
        cst = sb("cst", [P, C_ALL])
        ident = cst[:, C_IDENT:C_IDENT + P]
        gates = sb("gates", [P, TOPK, NJ])
        mx = sb("mx", [P, TOPK, NJ])
        dst_i = sb("dst_i", [P, NC], I32)
        src_i = sb("src_i", [P, NC + TB], I32)
        e_idx = sb("e_idx", [1, NS], I32)
        ones8 = sb("ones8", [P, E])
        b2_all = sb("b2_all", [P, E, D])
        b1_all = sb("b1_all", [P, E, FB])
        grid = sb("grid", [P, 5, KD, D])
        gr = sb("gr", [P, 3, KD * D])
        dt_b = sb("dt_b", [P, NB])

        with ExitStack() as phase:
            def own(name, shape, dt_=F32):
                return phase.enter_context(nc.sbuf_tensor(name, shape, dt_))

            raw_a = own("raw_a", [P, 2, 2048])
            raw_b = own("raw_b", [P, 2, 2048])
            w_split = own("w_split", [P, 2, 2, 2, 2048], F32R)
            hid = own("hid", [P, 2, 2, FB, ST], F32R)
            relu = own("relu", [P, 2, 2, ST])
            slot_h = own("slot_h", [P, 2, 2, KD, ST], F32R)
            gathered = own("gathered", [P, 2, TB, D])
            y_sb = own("y_sb", [P, 2, TB, D])
            b1_cur = own("b1_cur", [P, 2, FB])
            src_cur = own("src_cur", [P, 2, TB], I32)
            dst_cur = own("dst_cur", [P, 2, TB], I32)
        w1_raw = [raw_a[:, i, :] for i in range(2)]
        w2_raw = [raw_b[:, i, :] for i in range(2)]

        with ExitStack() as phase:
            def own(name, shape, dt_=F32):
                return phase.enter_context(nc.sbuf_tensor(name, shape, dt_))

            h_pre = own("h_pre", [P, KD, N])
            hT = own("hT", [P, KD, N])
            own("w_split_first", [P, 10240])
            z = own("z", [P, 4, D])
            tok = own("tok", [P, TOPK * NJ, 2, NC], BF16)
            oh_row = own("oh_row", [P, 4, P], BF16)
            own("w_split_last", [P, 6144 - 1024 - TOPK * NJ * NC - 256])
            h_tok = own("h_tok", [P, NJ, D])
            oh_col = own("oh_col", [P, TOPK * NJ, NC], BF16)
            before_bf = own("before_bf", [P, P], BF16)
            ones_bf = own("ones_bf", [P, P], BF16)
            row_bf = own("row_bf", [P, P], BF16)
            st1 = own("st1", [P, NJ, 6])
            mv1 = own("mv1", [P, NJ, 2])
            var1 = own("var1", [P, NJ])
            rs1 = own("rs1", [P, NJ])
            st2 = own("st2", [P, NB, KD, 6])
            mv2 = own("mv2", [P, NB, KD, 2])
            var2 = own("var2", [P, NB, KD])
            rs2 = own("rs2", [P, NB, KD])
            half = own("half", [P, 8])
            aff_a = own("aff_a", [P, NB, KD])
            aff_m = own("aff_m", [P, NB, KD])
            aff_b = own("aff_b", [P, NB, KD])
            id_i = own("id_i", [S_SUB, NB], I32)
            id_f = own("id_f", [S_SUB, NB])
            oh_s = own("oh_s", [S_SUB, NB])
            small_sb = own("small_sb", [P, SMALL_ALL])
            se_t = own("se_t", [SE, NB])
            hy1 = own("hy1", [SH, NB])
            hy2 = own("hy2", [SH, NB])
            sy1 = own("sy1", [SH // 2, NB])
            sty = own("sty", [P, 4, NB])
            gabs = own("gabs", [P, KD, NB])
            grelu = own("grelu", [P, KD, NB])
            gexp = own("gexp", [P, KD, NB])
            gln = own("gln", [P, KD, NB])
            gsum = own("gsum", [P, KD, NB])
            gam = own("gam", [P, KD, NB])
            lg = own("lg", [P, NJ, E])
            eq = own("eq", [P, NJ, E])
            cand = own("cand", [P, NJ, E])
            least = own("least", [P, NJ])
            choice = own("choice", [P, TOPK, NJ])
            oh = own("oh", [P, TOPK, NJ, E])
            lg2 = own("lg2", [P, NJ, E])
            gap = own("gap", [P, NJ])
            e2 = own("e2", [P, NJ])
            den = own("den", [P, NJ])
            m_bf = own("m_bf", [P, NJ, E], BF16)
            cnt_i = own("cnt_i", [P, E], I32)
            tl_i = own("tl_i", [P, E], I32)
            tl_f = own("tl_f", [P, E])
            t_end = own("t_end", [P, E])
            t_off = own("t_off", [P, E])
            base = own("base", [P, E])
            pos = own("pos", [P, NJ, E])
            pick = own("pick", [P, TOPK, NJ, E])
            slot_f = own("slot_f", [P, TOPK * NJ])
            slot_i = own("slot_i", [P, TOPK * NJ], I32)
            low_i = own("low_i", [P, TOPK * NJ], I32)
            col_i = own("col_i", [P, TOPK * NJ], I32)
            low_f = own("low_f", [P, TOPK * NJ])
            col_f = own("col_f", [P, TOPK * NJ])
            e_cmp = own("e_cmp", [1, NS, E])
            e_sum = own("e_sum", [1, NS])
            num = own("num", [P, NC])
            num_e = own("num_e", [P, NC])
            num_f = own("num_f", [P, NC])
            dst_f = own("dst_f", [P, NC])

        def part(name):
            rows, cols, at = SMALL[name]
            return small_sb[0:rows, at:at + cols]

        rw_sb = part("router_w").rearrange("p (k e) -> p k e", k=KD)
        emb, hw1, hw2, sw1, sw2 = (part(n) for n in ("subj_emb", "hyp_w1", "hyp_w2", "sty_w1", "sty_w2"))
        hb1, hb2, sbi1, sbi2 = (part(n) for n in ("hyp_b1", "hyp_b2", "sty_b1", "sty_b2"))
        ln_gain, ln_offset = part("ln_g"), part("ln_b")

        with ExitStack() as phase:
            def own(name, shape, dt_=F32):
                return phase.enter_context(nc.sbuf_tensor(name, shape, dt_))

            Y1, Y2, FV, F0, PA, PB, CC, U1, U2, PP, PQ, PR, SM, TT, OUT = (
                [own(f"{n}_{par}", [P, 4 * D])[:, :] for par in range(2)]
                for n in ("t_y1", "t_y2", "t_f", "t_f0", "t_a0f", "t_b2f", "t_d1b2f", "t_u1", "t_b0f", "t_pf",
                          "t_qf", "t_b1f", "t_cols", "t_new", "t_out"))
            edge_w = own("edge_w", [P, 2, KD, 8])
            edge_t = own("edge_t", [P, KD, 8])
            edge_p = own("edge_p", [P, 2, 2, 4, 2, 4])

        x_in = [sem(f"x_in{i}") for i in range(4)]
        cst_in = sem("cst_in")
        sty_in = sem("sty_in")
        exp_in = sem("exp_in")
        grid_in = sem("grid_in")
        chain = sem("chain")
        half_set = sem("half_set")
        var1_ok = sem("var1_ok")
        rs1_ok = sem("rs1_ok")
        z_ok = sem("z_ok")
        fwd_t = sem("fwd_t")
        pre_ok = sem("pre_ok")
        var2_ok = sem("var2_ok")
        rs2_ok = sem("rs2_ok")
        ht_ok = sem("ht_ok")
        logits_ok = sem("logits_ok")
        back_t = sem("back_t")
        htok_ok = sem("htok_ok")
        hrows_out = sem("hrows_out")
        sty_pe = sem("sty_pe")
        sty_act = sem("sty_act")
        sty_dve = sem("sty_dve")
        gap_ok = sem("gap_ok")
        e2_ok = sem("e2_ok")
        m_ok = sem("m_ok")
        rank_ok = sem("rank_ok")
        tok_ok = sem("tok_ok")
        ohrow_ok = sem("ohrow_ok")
        perm_mm = sem("perm_mm")
        e_ok = sem("e_ok")
        w1_in = [sem(f"w1_in{i}") for i in range(2)]
        w2_in = [sem(f"w2_in{i}") for i in range(2)]
        w1_hi, w1_lo, w2_hi, w2_lo = sem("w1_hi"), sem("w1_lo"), sem("w2_hi"), sem("w2_lo")
        h_hi, h_lo = sem("h_hi"), sem("h_lo")
        b1_ok = sem("b1_ok")
        l1_done, relu_ok, hid_hi, hid_lo, l2_done = (sem("l1_done"), sem("relu_ok"), sem("hid_hi"),
                                                     sem("hid_lo"), sem("l2_done"))
        pool_go = sem("pool_go")
        tr_done, y_ok = sem("tr_done"), sem("y_ok")
        src_ok, dst_ok = sem("src_ok"), sem("dst_ok")
        rows_in = [sem(f"rows_in{i}") for i in range(2)]
        y_out = [sem(f"y_out{i}") for i in range(2)]

        y_in = [sem(f"y_in{i}") for i in range(2)]
        t_first, t_f, t_a, t_b, t_u2, t_p, t_q, t_r = (sem(n) for n in (
            "t_first", "t_f", "t_a", "t_b", "t_u2", "t_p", "t_q", "t_r"))
        t_u1, t_sum, t_mm, t_fin, t_relu = (sem(n) for n in ("t_u1", "t_sum", "t_mm", "t_fin", "t_relu"))
        out_dma = [sem(f"out_dma{i}") for i in range(2)]
        grids_ok = sem("grids_ok")

        x_tok = x.rearrange("b (q p) d -> p (b q) d", p=P)
        out_tok = out.rearrange("b (q p) d -> p (b q) d", p=P)
        h_rows_tok = h_rows.rearrange("(j p) d -> p j d", p=P)
        y_rows_tok = y_rows.rearrange("(c j p) d -> c p j d", c=TOPK, p=P)
        w1_of = exp_w1.rearrange("e (k p) f -> p e k f", p=P)
        w2_of = exp_w2.rearrange("e (p b) d -> p e (b d)", b=FB)

        block = ctx.enter_context(nc.Block())

        NPAIR = NB // 2
        LOOP = range(1, (NS - 1) // 2)
        assert NS % 2 == 1

        @block.sync
        def _(sp):
            for i in range(4):
                sp.dma_start(x_sb[:, 4 * i:4 * i + 4, :], x_tok[:, 4 * i:4 * i + 4, :]).then_inc(x_in[i], 16)
            for b in range(NB):
                sp.wait_ge(htok_ok, b + 1)
                sp.dma_start(h_rows_tok[:, 2 * b:2 * b + 2, :], h_tok[:, 2 * b:2 * b + 2, :]).then_inc(hrows_out, 16)

            def weights(s, par, ring):
                e = sp.value_load(e_idx[0:1, bass.DynSlice(s, 1)], min_val=0, max_val=E - 1)
                if ring:
                    sp.wait_ge(w1_hi, s - 1)
                    sp.wait_ge(w1_lo, s - 1)
                sp.dma_start(w1_raw[par].rearrange("p (k f) -> p k f", k=KD),
                             w1_of[:, bass.DynSlice(e, 1), :, :].rearrange("p e k f -> p (e k) f")
                             ).then_inc(w1_in[par], 16)
                if ring:
                    sp.wait_ge(w2_hi, s - 1)
                    sp.wait_ge(w2_lo, s - 1)
                sp.dma_start(w2_raw[par], w2_of[:, bass.DynSlice(e, 1), :].rearrange("p e n -> p (e n)")
                             ).then_inc(w2_in[par], 16)

            sp.wait_ge(e_ok, 1)
            sp.wait_ge(back_t, NB)
            weights(0, 0, False)
            weights(1, 1, False)
            with sp.Fori(1, LOOP.stop) as m:
                for par in range(2):
                    weights(2 * m + par, par, True)
            weights(NS - 1, 0, True)

            sp.wait_ge(l2_done, NS)
            for par in range(2):
                sp.wait_ge(y_out[par], 32 * ((NS + 1 - par) // 2))
            for g in range(NPAIR):
                if g >= 2:
                    sp.wait_ge(t_f, g - 1)
                for c, buf in enumerate((Y1, Y2)):
                    sp.dma_start(buf[g % 2].rearrange("p (j d) -> p j d", j=4),
                                 y_rows_tok[c, :, 4 * g:4 * g + 4, :]).then_inc(y_in[g % 2], 16)
            for g in range(NPAIR):
                sp.wait_ge(t_relu, g + 1)
                sp.dma_start(out_tok[:, 4 * g:4 * g + 4, :],
                             OUT[g % 2].rearrange("p (j d) -> p j d", j=4)).then_inc(out_dma[g % 2], 16)
            for par in range(2):
                sp.wait_ge(out_dma[par], 16 * (NPAIR // 2))
            sp.wait_ge(hrows_out, 16 * NB)

        @block.scalar
        def _(act):
            def load(dst, src, s):
                act.dma_start(dst, src).then_inc(s, 16)

            load(cst[:, :], consts, cst_in)
            load(small_sb[:, :], small, sty_in)
            load(id_i[:, :], ids.rearrange("(a b) -> a b", a=1).partition_broadcast(S_SUB), sty_in)
            load(b1_all[:, :, :], exp_b1.rearrange("e (p b) -> p e b", b=FB), exp_in)
            load(b2_all[:, :, :], exp_b2.rearrange("(a e) d -> a e d", a=1).partition_broadcast(P), exp_in)
            load(grid[:, 0:2, :, :], a_grid.rearrange("g (q p) d -> p g q d", p=P), grid_in)
            load(grid[:, 2:5, :, :], b_grid.rearrange("g (q p) d -> p g q d", p=P), grid_in)
            load(dt_b[:, :], dt.rearrange("(a b) -> a b", a=1).partition_broadcast(P), grid_in)

            act.wait_ge(sty_in, 32)
            act.wait_ge(sty_pe, 1)
            act.activation(se_t[:, :], banks[1][0:SE, 0:NB], ACT.Copy).then_inc(sty_act, 1)
            act.wait_ge(sty_pe, 2)
            act.activation(hy1[:, :], banks[1][:, 8:8 + NB], ACT.Relu, bias=hb1[:, 0:1]).then_inc(sty_act, 1)
            act.wait_ge(sty_pe, 3)
            act.activation(hy2[:, :], banks[1][:, 16:16 + NB], ACT.Identity, bias=hb2[:, 0:1]).then_inc(sty_act, 1)
            act.wait_ge(sty_pe, 4)
            act.activation(sy1[:, :], banks[1][0:SH // 2, 24:24 + NB], ACT.Relu,
                           bias=sbi1[:, 0:1]).then_inc(sty_act, 1)
            act.wait_ge(sty_pe, 5)
            for c in range(4):
                last = act.activation(sty[:, c, :], banks[1][:, 32 + 8 * c:40 + 8 * c], ACT.Identity,
                                      bias=sbi2[:, c:c + 1])
            last.then_inc(sty_act, 1)
            act.wait_ge(sty_act, 5)
            act.activation(gabs[:, :, :], sty[:, 0:KD, :], ACT.Abs).then_inc(sty_act, 1)
            act.wait_ge(sty_act, 6)
            act.activation(gexp[:, :, :], gabs[:, :, :], ACT.Exp, scale=-1.0).then_inc(sty_act, 1)
            act.wait_ge(sty_act, 7)
            act.activation(gln[:, :, :], gexp[:, :, :], ACT.Ln, bias=ones8[:, 0:1]).then_inc(sty_act, 1)

            def front(b):
                act.wait_ge(fwd_t, b + 1)
                for k in range(KD):
                    last = act.activation(h_pre[:, k, T * b:T * b + T], banks[4 + b % 2][:, T * k:T * k + T],
                                          ACT.Identity, bias=ln_offset[:, k:k + 1], scale=ln_gain[:, k:k + 1])
                last.then_inc(pre_ok, 1)

            def rows(b):
                act.wait_ge(back_t, b + 1)
                act.activation(h_tok[:, 2 * b:2 * b + 2, :],
                               banks[6 + b % 2][:, :].rearrange("p (j d) -> p j d", j=2),
                               ACT.Copy).then_inc(htok_ok, 1)

            for b in range(NB + 2):
                if b < NB:
                    front(b)
                if b >= 2:
                    rows(b - 2)

            act.wait_ge(gap_ok, 1)
            act.activation(e2[:, :], gap[:, :], ACT.Exp).then_inc(e2_ok, 1)

            def split_w1(s, par, landed, first=False):
                act.wait_ge(w1_in[par], landed)
                if not first:
                    act.wait_ge(l1_done, BANKS * (s - 1))
                act.activation(w_split[:, 0, par, 0, :].rearrange("p (k b f) -> p k b f", k=KD, b=FB),
                               w1_raw[par].rearrange("p (k f b) -> p k b f", k=KD, b=FB),
                               ACT.Copy).then_inc(w1_hi, 1)

            def split_w2(s, par, landed, first=False):
                act.wait_ge(w2_in[par], landed)
                if not first:
                    act.wait_ge(l2_done, s - 1)
                act.activation(w_split[:, 1, par, 0, :], w2_raw[par], ACT.Copy).then_inc(w2_hi, 1)

            def split_h(s, par, first=False):
                act.wait_ge(tr_done, s + 1)
                if not first:
                    act.wait_ge(l1_done, BANKS * (s - 1))
                act.activation(slot_h[:, par, 0, :, :], banks[6][:, :].rearrange("p (k n) -> p k n", k=KD),
                               ACT.Copy).then_inc(h_hi, 1)

            def step(s, par, landed, begin=BANKS, last_slot=False):
                e = act.value_load(e_idx[0:1, bass.DynSlice(s, 1)], min_val=0, max_val=E - 1)
                act.activation(b1_cur[:, par, :],
                               b1_all[:, bass.DynSlice(e, 1), :].rearrange("p e b -> p (e b)"),
                               ACT.Copy).then_inc(b1_ok, 1)
                act.wait_ge(b1_ok, s + 1)
                for bank in range(BANKS):
                    act.wait_ge(l1_done, BANKS * s + bank + 1)
                    if begin > 0 or bank >= 2:
                        act.wait_ge(hid_lo, BANKS * s + bank - 1)
                    for i in range(2):
                        blk = 2 * bank + i
                        last = act.activation(relu[:, bank % 2, i, :], banks[bank][:, ST * i:ST * i + ST],
                                              ACT.Relu, bias=b1_cur[:, par, blk:blk + 1])
                    last.then_inc(relu_ok, 1)
                if not last_slot:
                    split_w1(s + 1, 1 - par, landed + 16 * par, first=begin == 0)
                    split_h(s + 1, 1 - par, first=begin == 0)
                split_w2(s, par, landed, first=begin < 2)

            act.wait_ge(exp_in, 32)
            act.wait_ge(e_ok, 1)
            split_w1(0, 0, 16, first=True)
            split_h(0, 0, first=True)
            step(0, 0, 16, begin=0)
            step(1, 1, 16, begin=1)
            with act.Fori(1, LOOP.stop) as m:
                for par in range(2):
                    step(2 * m + par, par, 16 * m + 16)
            step(NS - 1, 0, 16 * ((NS - 1) // 2) + 16, last_slot=True)

            for g in range(NPAIR):
                act.wait_ge(t_fin, g + 1)
                if g >= 2:
                    act.wait_ge(out_dma[g % 2], 16 * (g // 2))
                act.activation(OUT[g % 2], TT[g % 2], ACT.Relu).then_inc(t_relu, 1)

        @block.gpsimd
        def _(pool):
            pool.memset(half[:, :], -0.5).then_inc(half_set, 1)
            pool.wait_ge(half_set, 1)
            for i in range(NB + 2):
                if i < NB:
                    pool.wait_ge(var1_ok, i + 1)
                    pool.tensor_tensor(rs1[:, 2 * i:2 * i + 2], var1[:, 2 * i:2 * i + 2], half[:, 0:2],
                                       ALU.pow).then_inc(rs1_ok, 1)
                if i >= 2:
                    pool.wait_ge(var2_ok, i - 1)
                    pool.tensor_tensor(rs2[:, i - 2, :], var2[:, i - 2, :], half[:, 0:KD],
                                       ALU.pow).then_inc(rs2_ok, 1)

            def gather(s, par, ring):
                pool.wait_ge(src_ok, s + 1)
                if ring:
                    pool.wait_ge(tr_done, s - 1)
                pool.sem_inc(pool_go, 1)
                for t in range(TB):
                    pool.indirect_dma_start(
                        out=gathered[:, par, t, :], out_offset=None, in_=h_rows,
                        in_offset=bass.IndirectOffsetOnAxis(ap=src_cur[:, par, t:t + 1], axis=0),
                    ).then_inc(rows_in[par], 16)

            def scatter(s, par):
                pool.wait_ge(y_ok, s + 1)
                pool.wait_ge(dst_ok, s + 1)
                pool.sem_inc(pool_go, 1)
                for t in range(TB):
                    pool.indirect_dma_start(
                        out=y_rows, out_offset=bass.IndirectOffsetOnAxis(ap=dst_cur[:, par, t:t + 1], axis=0),
                        in_=y_sb[:, par, t, :], in_offset=None, bounds_check=TOPK * N - 1, oob_is_err=False,
                    ).then_inc(y_out[par], 16)

            def high(s, par, ring):
                for bank in range(BANKS):
                    pool.wait_ge(relu_ok, BANKS * s + bank + 1)
                    if ring and bank == 0:
                        pool.wait_ge(l2_done, s - 1)
                    pool.sem_inc(pool_go, 1)
                    pool.tensor_scalar(hid[:, par, 0, 2 * bank:2 * bank + 2, :], relu[:, bank % 2, :, :],
                                       1.0, 0.0, ALU.mult, ALU.add).then_inc(hid_hi, 1)

            pool.wait_ge(hrows_out, 16 * NB)
            gather(0, 0, False)
            gather(1, 1, False)
            for s in range(2):
                gather(s + 2, s, True)
                high(s, s, False)
            with pool.Fori(1, LOOP.stop) as m:
                for par in range(2):
                    s = 2 * m + par
                    gather(s + 2, par, True)
                    high(s, par, True)
                    scatter(s - 2, par)
            high(NS - 1, 0, True)
            scatter(NS - 3, 0)
            scatter(NS - 2, 1)
            scatter(NS - 1, 0)

            for g in range(NPAIR):
                f = FV[g % 2].rearrange("p (i n) -> p i n", i=2)
                pool.wait_ge(t_f, g + 1)
                pool.wait_ge(grids_ok, 1)
                if g >= 2:
                    pool.wait_ge(t_sum, g - 1)
                    pool.wait_ge(t_mm, g - 1)
                pool.tensor_tensor(U2[g % 2].rearrange("p (i n) -> p i n", i=2),
                                   grid[:, 2, :, :].rearrange("p (a q) d -> p a (q d)", a=1).broadcast_to([P, 2, 512]),
                                   f, ALU.mult).then_inc(t_u2, 1)
                pool.tensor_tensor(PP[g % 2].rearrange("p (i n) -> p i n", i=2),
                                   gr[:, 0:1, :].broadcast_to([P, 2, 512]), f, ALU.mult).then_inc(t_p, 1)
                pool.tensor_tensor(PQ[g % 2].rearrange("p (i n) -> p i n", i=2),
                                   gr[:, 1:2, :].broadcast_to([P, 2, 512]), f, ALU.mult).then_inc(t_q, 1)

        @block.tensor
        def _(pe):
            pe.wait_ge(sty_in, 32)
            pe.wait_ge(sty_dve, 1)
            pe.matmul(banks[1][0:SE, 0:NB], emb[:, :], oh_s[:, :], start=True, stop=True).then_inc(sty_pe, 1)
            pe.wait_ge(sty_act, 1)
            pe.matmul(banks[1][:, 8:8 + NB], hw1[:, :], se_t[:, :], start=True, stop=True).then_inc(sty_pe, 1)
            pe.wait_ge(sty_act, 2)
            pe.matmul(banks[1][:, 16:16 + NB], hw2[:, :], hy1[:, :], start=True, stop=True).then_inc(sty_pe, 1)
            pe.wait_ge(sty_act, 3)
            pe.matmul(banks[1][0:SH // 2, 24:24 + NB], sw1[:, :], hy2[:, :], start=True, stop=True).then_inc(sty_pe, 1)
            pe.wait_ge(sty_act, 4)
            for c in range(4):
                last = pe.matmul(banks[1][:, 32 + 8 * c:40 + 8 * c], sw2[:, P * c:P * c + P], sy1[:, :],
                                 start=True, stop=True)
            last.then_inc(sty_pe, 1)

            pe.wait_ge(cst_in, 16)

            def forward(b):
                pe.wait_ge(z_ok, b + 1)
                if b >= 2:
                    pe.wait_ge(pre_ok, b - 1)
                for k in range(KD):
                    for q in range(2):
                        last = pe.transpose(banks[4 + b % 2][:, T * k + P * q:T * k + P * q + P],
                                            z[:, (2 * b + q) % 4, P * k:P * k + P], ident)
                last.then_inc(fwd_t, 1)

            def route_and_back(b):
                pe.wait_ge(ht_ok, b + 1)
                for j in range(2 * b, 2 * b + 2):
                    for k in range(KD):
                        last = pe.matmul(banks[0][:, E * j:E * j + E], hT[:, k, P * j:P * j + P], rw_sb[:, k, :],
                                         start=(k == 0), stop=(k == KD - 1))
                last.then_inc(logits_ok, 1)
                if b >= 2:
                    pe.wait_ge(htok_ok, b - 1)
                for q in range(2):
                    for k in range(KD):
                        last = pe.transpose(banks[6 + b % 2][:, D * q + P * k:D * q + P * k + P],
                                            hT[:, k, T * b + P * q:T * b + P * q + P], ident)
                last.then_inc(back_t, 1)

            for i in range(NB + 2):
                if i < NB:
                    forward(i)
                if i >= 2:
                    route_and_back(i - 2)

            pe.wait_ge(m_ok, 1)
            rank = banks[2][:, 0:NJ * E]
            for j in range(NJ):
                pe.matmul(rank[:, E * j:E * j + E], before_bf[:, :], m_bf[:, j, :], start=True, stop=(j == 0))
                for i in range(j):
                    pe.matmul(rank[:, E * j:E * j + E], ones_bf[:, :], m_bf[:, i, :], start=False,
                              stop=(i == j - 1))
            for j in range(NJ):
                last = pe.matmul(banks[3][:, 0:E], ones_bf[:, :], m_bf[:, j, :], start=(j == 0), stop=(j == NJ - 1))
            last.then_inc(rank_ok, 1)

            pe.wait_ge(tok_ok, 1)
            for t in range(TOPK * NJ):
                pe.wait_ge(ohrow_ok, t + 1)
                pe.matmul(banks[1][:, 128:128 + 2 * NC], oh_row[:, t % 4, :],
                          tok[:, t, :, :].rearrange("p a n -> p (a n)"),
                          start=(t == 0), stop=(t == TOPK * NJ - 1)).then_inc(perm_mm, 1)

            def turn(s, par, mr, first=False):
                pe.wait_ge(rows_in[par], mr)
                if not first:
                    pe.wait_ge(h_hi, s)
                    pe.wait_ge(h_lo, s)
                for k in range(KD):
                    for t in range(TB):
                        last = pe.transpose(banks[6][:, ST * k + P * t:ST * k + P * t + P],
                                            gathered[:, par, t, P * k:P * k + P], ident)
                last.then_inc(tr_done, 1)

            PARTS = ((0, 0), (0, 1), (1, 0))

            def layer1(s, par, first=False):
                pe.wait_ge(w1_hi, s + 1)
                pe.wait_ge(w1_lo, s + 1)
                pe.wait_ge(h_hi, s + 1)
                pe.wait_ge(h_lo, s + 1)
                for blk in range(FB):
                    bank = blk // 2
                    if blk % 2 == 0 and not first:
                        pe.wait_ge(relu_ok, BANKS * s + bank - 3)
                    n = 0
                    for k in range(KD):
                        for w, h in PARTS:
                            at = (k * FB + blk) * P
                            last = pe.matmul(banks[bank][:, ST * (blk % 2):ST * (blk % 2) + ST],
                                             w_split[:, 0, par, w, at:at + P], slot_h[:, par, h, k, :],
                                             start=(n == 0), stop=(n == 3 * KD - 1))
                            n += 1
                    if blk % 2:
                        last.then_inc(l1_done, 1)

            def layer2(s, par, ring):
                pe.wait_ge(w2_hi, s + 1)
                pe.wait_ge(w2_lo, s + 1)
                pe.wait_ge(hid_lo, BANKS * (s + 1))
                if ring:
                    pe.wait_ge(y_ok, s - 1)
                for t in range(TB):
                    n = 0
                    for blk in range(FB):
                        for w, h in PARTS:
                            last = pe.matmul(banks[4 + par][:, D * t:D * t + D],
                                             hid[:, par, h, blk, P * t:P * t + P],
                                             w_split[:, 1, par, w, D * blk:D * blk + D],
                                             start=(n == 0), stop=(n == 3 * FB - 1))
                            n += 1
                last.then_inc(l2_done, 1)

            turn(0, 0, 32, first=True)
            layer1(0, 0, first=True)
            turn(1, 1, 32)
            layer1(1, 1)
            turn(2, 0, 64)
            layer2(0, 0, False)
            layer1(2, 0)
            turn(3, 1, 64)
            layer2(1, 1, False)
            with pe.Fori(1, LOOP.stop) as m:
                layer1(2 * m + 1, 1)
                turn(2 * m + 2, 0, 32 * m + 64)
                layer2(2 * m, 0, True)
                layer1(2 * m + 2, 0)
                turn(2 * m + 3, 1, 32 * m + 64)
                layer2(2 * m + 1, 1, True)
            layer2(NS - 1, 0, True)

            for g in range(NPAIR):
                pe.wait_ge(t_u1, g + 1)
                pe.wait_ge(t_u2, g + 1)
                if g >= 2:
                    pe.wait_ge(t_fin, g - 1)
                for q in range(2):
                    n = 0
                    for col, u in ((C_D1, U1[g % 2]), (C_D2, U2[g % 2])):
                        uv = u.rearrange("p (i q d) -> p q i d", i=2, q=2)
                        for k in range(2):
                            last = pe.matmul(banks[2 * (g % 2) + q][:, :].rearrange("p (i d) -> p i d", i=2),
                                             cst[:, col + T * k + P * q:col + T * k + P * q + P], uv[:, k, :, :],
                                             start=(n == 0), stop=(n == 3))
                            n += 1
                last.then_inc(t_mm, 1)

        @block.vector
        def _(dve):
            steps = [0]

            def link(ins):
                steps[0] += 1
                ins.then_inc(chain, 1)
                dve.wait_ge(chain, steps[0])

            dve.memset(ones_bf[:, :], 1.0)
            link(dve.memset(ones8[:, :], 1.0))
            dve.wait_ge(cst_in, 16)
            dve.tensor_copy(before_bf[:, :], cst[:, C_BEFORE:C_BEFORE + P])
            link(dve.tensor_copy(row_bf[:, :], cst[:, C_ROW:C_ROW + P]))
            dve.wait_ge(sty_in, 32)
            link(dve.tensor_copy(id_f[:, :], id_i[:, :]))
            dve.tensor_scalar(oh_s[:, :], id_f[:, :], cst[0:S_SUB, C_PART:C_PART + 1], None,
                              ALU.is_equal).then_inc(sty_dve, 1)

            def stats(b):
                if b % 2 == 0:
                    dve.wait_ge(x_in[b // 2], 16)
                for j in range(2 * b, 2 * b + 2):
                    last = dve.bn_stats(st1[:, j, :], x_sb[:, j, :])
                link(last)
                for j in range(2 * b, 2 * b + 2):
                    last = dve.bn_aggr(mv1[:, j, :], st1[:, j, :])
                link(last)
                dve.tensor_scalar(var1[:, 2 * b:2 * b + 2], mv1[:, 2 * b:2 * b + 2, 1], 1e-5, None,
                                  ALU.add).then_inc(var1_ok, 1)

            def normed(b):
                dve.wait_ge(rs1_ok, b + 1)
                if b >= 2:
                    dve.wait_ge(fwd_t, b - 1)
                for j in range(2 * b, 2 * b + 2):
                    last = dve.tensor_scalar(z[:, j % 4, :], x_sb[:, j, :], mv1[:, j, 0:1], rs1[:, j:j + 1],
                                             ALU.subtract, ALU.mult)
                last.then_inc(z_ok, 1)

            def time_stats(b):
                dve.wait_ge(pre_ok, b + 1)
                for k in range(KD):
                    last = dve.bn_stats(st2[:, b, k, :], h_pre[:, k, T * b:T * b + T])
                link(last)
                for k in range(KD):
                    last = dve.bn_aggr(mv2[:, b, k, :], st2[:, b, k, :])
                link(last)
                dve.tensor_scalar(var2[:, b, :], mv2[:, b, :, 1], 1e-8, None, ALU.add).then_inc(var2_ok, 1)

            def styled(b):
                dve.wait_ge(rs2_ok, b + 1)
                link(dve.tensor_tensor(aff_a[:, b, :], rs2[:, b, :], gam[:, :, b], ALU.mult))
                link(dve.tensor_tensor(aff_m[:, b, :], mv2[:, b, :, 0], aff_a[:, b, :], ALU.mult))
                link(dve.tensor_tensor(aff_b[:, b, :], sty[:, KD:2 * KD, b], aff_m[:, b, :], ALU.subtract))
                for k in range(KD):
                    last = dve.tensor_scalar(hT[:, k, T * b:T * b + T], h_pre[:, k, T * b:T * b + T],
                                             aff_a[:, b, k:k + 1], aff_b[:, b, k:k + 1], ALU.mult, ALU.add)
                last.then_inc(ht_ok, 1)

            for i in range(NB + 3):
                if i < NB:
                    stats(i)
                if 1 <= i < NB + 1:
                    normed(i - 1)
                if i == 2:
                    dve.wait_ge(sty_act, 8)
                    link(dve.tensor_scalar(grelu[:, :, :], sty[:, 0:KD, :], 0.0, None, ALU.max))
                    link(dve.tensor_tensor(gsum[:, :, :], grelu[:, :, :], gln[:, :, :], ALU.add))
                    link(dve.tensor_scalar(gam[:, :, :], gsum[:, :, :], 1e-8, None, ALU.add))
                if 2 <= i < NB + 2:
                    time_stats(i - 2)
                if i >= 3:
                    styled(i - 3)

            dve.wait_ge(logits_ok, NB)
            link(dve.tensor_copy(lg[:, :, :], banks[0][:, 0:NJ * E].rearrange("p (j e) -> p j e", e=E)))
            expert = cst[:, C_EXPERT:C_EXPERT + NJ * E].rearrange("p (j e) -> p j e", e=E)

            def spread(v):
                return v.rearrange("p (j a) -> p j a", a=1).broadcast_to([P, NJ, E])

            for c, src in enumerate((lg, lg2)):
                link(dve.tensor_reduce(mx[:, c, :], src[:, :, :], AX_X, ALU.max))
                link(dve.tensor_tensor(eq[:, :, :], src[:, :, :], spread(mx[:, c, :]), ALU.is_equal))
                link(dve.scalar_tensor_tensor(out=cand[:, :, :], in0=eq[:, :, :], scalar=-float(E), in1=expert,
                                              op0=ALU.mult, op1=ALU.add))
                link(dve.tensor_reduce(least[:, :], cand[:, :, :], AX_X, ALU.min))
                link(dve.tensor_scalar(choice[:, c, :], least[:, :], float(E), None, ALU.add))
                link(dve.tensor_tensor(oh[:, c, :, :], expert, spread(choice[:, c, :]), ALU.is_equal))
                if c == 0:
                    link(dve.scalar_tensor_tensor(out=lg2[:, :, :], in0=oh[:, 0, :, :], scalar=-3e38,
                                                  in1=lg[:, :, :], op0=ALU.mult, op1=ALU.add))
            dve.tensor_tensor(gap[:, :], mx[:, 1, :], mx[:, 0, :], ALU.subtract).then_inc(gap_ok, 1)
            dve.tensor_tensor(m_bf[:, :, :], oh[:, 0, :, :], oh[:, 1, :, :], ALU.add).then_inc(m_ok, 1)

            dve.wait_ge(e2_ok, 1)
            link(dve.tensor_scalar(den[:, :], e2[:, :], 1.0, None, ALU.add))
            link(dve.reciprocal(gates[:, 0, :], den[:, :]))
            link(dve.tensor_tensor(gates[:, 1, :], e2[:, :], gates[:, 0, :], ALU.mult))

            dve.wait_ge(rank_ok, 1)
            link(dve.tensor_scalar(cnt_i[:, :], banks[3][:, 0:E], float(ST - 1), None, ALU.add))
            link(dve.tensor_scalar(tl_i[:, :], cnt_i[:, :], ST.bit_length() - 1, None, ALU.arith_shift_right))
            link(dve.tensor_copy(tl_f[:, :], tl_i[:, :]))
            link(dve.tensor_tensor_scan(t_end[:, :], ones8[:, :], tl_f[:, :], 0.0, ALU.mult, ALU.add))
            link(dve.tensor_tensor(t_off[:, :], t_end[:, :], tl_f[:, :], ALU.subtract))
            link(dve.tensor_tensor(e_cmp[:, :, :],
                                   t_off[0:1, :].rearrange("p (a e) -> p a e", a=1).broadcast_to([1, NS, E]),
                                   cst[0:1, C_SLOT:C_SLOT + NS * E].rearrange("p (s e) -> p s e", e=E), ALU.is_le))
            link(dve.tensor_reduce(e_sum[:, :], e_cmp[:, :, :], AX_X, ALU.add))
            dve.tensor_scalar(e_idx[:, :], e_sum[:, :], -1.0, None, ALU.add).then_inc(e_ok, 1)
            link(dve.tensor_scalar(base[:, :], t_off[:, :], float(ST), None, ALU.mult))
            link(dve.tensor_tensor(pos[:, :, :], banks[2][:, 0:NJ * E].rearrange("p (j e) -> p j e", e=E),
                                   base[:, :].rearrange("p (a e) -> p a e", a=1).broadcast_to([P, NJ, E]), ALU.add))
            for c in range(TOPK):
                link(dve.tensor_tensor(pick[:, c, :, :], pos[:, :, :], oh[:, c, :, :], ALU.mult))
                link(dve.tensor_reduce(slot_f[:, NJ * c:NJ * c + NJ], pick[:, c, :, :], AX_X, ALU.add))
            link(dve.tensor_copy(slot_i[:, :], slot_f[:, :]))
            link(dve.tensor_scalar(low_i[:, :], slot_i[:, :], P - 1, None, ALU.bitwise_and))
            link(dve.tensor_scalar(col_i[:, :], slot_i[:, :], P.bit_length() - 1, None, ALU.arith_shift_right))
            link(dve.tensor_copy(low_f[:, :], low_i[:, :]))
            link(dve.tensor_copy(col_f[:, :], col_i[:, :]))
            link(dve.tensor_tensor(
                oh_col[:, :, :],
                col_f[:, :].rearrange("p (t a) -> p t a", a=1).broadcast_to([P, TOPK * NJ, NC]),
                cst[:, C_COL:C_COL + NC].rearrange("p (a n) -> p a n", a=1).broadcast_to([P, TOPK * NJ, NC]),
                ALU.is_equal))
            dve.tensor_scalar(tok[:, :, 0, :], oh_col[:, :, :], cst[:, C_PART + 1:C_PART + 2], None, ALU.mult)
            dve.tensor_tensor(
                tok[:, :, 1, :], oh_col[:, :, :],
                cst[:, C_JC:C_JC + TOPK * NJ].rearrange("p (t a) -> p t a", a=1).broadcast_to([P, TOPK * NJ, NC]),
                ALU.mult).then_inc(tok_ok, 1)
            for t in range(TOPK * NJ):
                if t >= 4:
                    dve.wait_ge(perm_mm, t - 3)
                dve.tensor_scalar(oh_row[:, t % 4, :], row_bf[:, :], low_f[:, t:t + 1], None,
                                  ALU.is_equal).then_inc(ohrow_ok, 1)
            dve.wait_ge(perm_mm, TOPK * NJ)
            parts = banks[1][:, 128:128 + 2 * NC]
            link(dve.tensor_copy(num_e[:, :], parts[:, 0:NC]))
            link(dve.scalar_tensor_tensor(out=num[:, :], in0=parts[:, NC:2 * NC], scalar=float(P), in1=num_e[:, :],
                                          op0=ALU.mult, op1=ALU.add))
            link(dve.tensor_scalar(num_e[:, :], num[:, :], 0.0, EMPTY, ALU.is_equal, ALU.mult))
            link(dve.scalar_tensor_tensor(out=dst_f[:, :], in0=num[:, :], scalar=-1.0, in1=num_e[:, :],
                                          op0=ALU.add, op1=ALU.add))
            link(dve.tensor_copy(dst_i[:, :], dst_f[:, :]))
            dve.memset(src_i[:, NC:NC + TB], 0)
            link(dve.tensor_scalar(src_i[:, 0:NC], dst_i[:, :], N - 1, None, ALU.bitwise_and))

            def source(s, par, ring):
                if ring is not None:
                    dve.wait_ge(rows_in[par], ring)
                dve.tensor_copy(src_cur[:, par, :], src_i[:, bass.DynSlice(TB * s, TB)]).then_inc(src_ok, 1)

            def low_w1(s, par):
                dve.wait_ge(w1_hi, s + 1)
                dve.tensor_tensor(w_split[:, 0, par, 1, :].rearrange("p (k b f) -> p (k b) f", k=KD, b=FB)
                                  .rearrange("p (k b) f -> p k b f", k=KD),
                                  w1_raw[par].rearrange("p (k f b) -> p k b f", k=KD, b=FB),
                                  w_split[:, 0, par, 0, :].rearrange("p (k b f) -> p k b f", k=KD, b=FB).bitcast(F32),
                                  ALU.subtract).then_inc(w1_lo, 1)

            def low_w2(s, par):
                dve.wait_ge(w2_hi, s + 1)
                dve.tensor_tensor(w_split[:, 1, par, 1, :], w2_raw[par], w_split[:, 1, par, 0, :].bitcast(F32),
                                  ALU.subtract).then_inc(w2_lo, 1)

            def low_h(s, par):
                dve.wait_ge(h_hi, s + 1)
                dve.tensor_tensor(slot_h[:, par, 1, :, :], banks[6][:, :].rearrange("p (k n) -> p k n", k=KD),
                                  slot_h[:, par, 0, :, :].bitcast(F32), ALU.subtract).then_inc(h_lo, 1)

            def low_hid(s, par):
                for bank in range(BANKS):
                    dve.wait_ge(hid_hi, BANKS * s + bank + 1)
                    dve.tensor_tensor(hid[:, par, 1, 2 * bank:2 * bank + 2, :], relu[:, bank % 2, :, :],
                                      hid[:, par, 0, 2 * bank:2 * bank + 2, :].bitcast(F32),
                                      ALU.subtract).then_inc(hid_lo, 1)

            def finish(s, par, ring):
                e = dve.value_load(e_idx[0:1, bass.DynSlice(s, 1)], min_val=0, max_val=E - 1)
                if ring is not None:
                    dve.wait_ge(y_out[par], ring)
                dve.tensor_copy(dst_cur[:, par, :], dst_i[:, bass.DynSlice(TB * s, TB)]).then_inc(dst_ok, 1)
                dve.wait_ge(l2_done, s + 1)
                dve.tensor_tensor(y_sb[:, par, :, :], banks[4 + par][:, :].rearrange("p (t d) -> p t d", t=TB),
                                  b2_all[:, bass.DynSlice(e, 1), :].broadcast_to([P, TB, D]),
                                  ALU.add).then_inc(y_ok, 1)

            source(0, 0, None)
            source(1, 1, None)
            low_w1(0, 0)
            low_h(0, 0)
            dve.wait_ge(exp_in, 32)
            def dve_step(s, par, gathered_by, scattered_by, first=False):
                source(s + 2, par, gathered_by)
                if not first:
                    finish(s - 2, par, scattered_by)
                low_hid(s, par)
                low_w1(s + 1, 1 - par)
                low_h(s + 1, 1 - par)
                low_w2(s, par)

            for s in range(4):
                dve_step(s, s % 2, 32 * (s // 2) + 32, None, first=s < 2)
            with dve.Fori(2, LOOP.stop) as m:
                for par in range(2):
                    dve_step(2 * m + par, par, 32 * m + 32, 32 * m - 32)
            last_round = (NS - 1) // 2
            finish(NS - 3, 0, 32 * (last_round - 1))
            low_hid(NS - 1, 0)
            low_w2(NS - 1, 0)
            finish(NS - 2, 1, 32 * (last_round - 1))
            finish(NS - 1, 0, 32 * last_round)

            dve.wait_ge(grid_in, 48)
            A0, A1, B0, B1, B2 = (grid[:, n, :, :].rearrange("p q d -> p (q d)") for n in range(5))
            dve.tensor_tensor(gr[:, 0, :], B1, A1, ALU.subtract)
            dve.tensor_tensor(gr[:, 1, :], B1, A1, ALU.add)
            link(dve.tensor_scalar(gr[:, 2, :], B2, 0.5, None, ALU.mult))
            dve.tensor_scalar(gr[:, 0:2, :], gr[:, 0:2, :], 0.5, None, ALU.mult).then_inc(grids_ok, 1)
            ew = cst[:, C_EDGE:C_EDGE + 24].rearrange("p (n c) -> p n c", n=3)

            def edge_cols(v):
                return v[:, :, 0:4], v[:, :, D - 4:D]

            for side in range(2):
                at = slice(4 * side, 4 * side + 4)
                for n, gi, dst in ((0, 3, edge_w[:, 0, :, at]), (1, 1, edge_t[:, :, at]), (2, 4, edge_w[:, 1, :, at])):
                    src = edge_cols(grid[:, gi, :, :])[side]
                    last = dve.tensor_tensor(
                        dst, src, ew[:, n:n + 1, at].broadcast_to([P, KD, 4]), ALU.mult)
            link(last)
            link(dve.tensor_tensor(edge_w[:, 0, :, :], edge_w[:, 0, :, :], edge_t[:, :, :], ALU.add))

            def add_up(g):
                dve.wait_ge(y_in[g % 2], 32 * (g // 2 + 1))
                y1, y2, f, f0 = (v[g % 2].rearrange("p (j d) -> p j d", j=4) for v in (Y1, Y2, FV, F0))
                if g >= 2:
                    dve.wait_ge(t_u2, g - 1)
                    dve.wait_ge(t_q, g - 1)
                for j in range(4):
                    last = dve.scalar_tensor_tensor(out=f0[:, j, :], in0=y1[:, j, :],
                                                    scalar=gates[:, 0, 4 * g + j:4 * g + j + 1],
                                                    in1=x_sb[:, 4 * g + j, :], op0=ALU.mult, op1=ALU.add)
                link(last)
                for j in range(4):
                    last = dve.scalar_tensor_tensor(out=f[:, j, :], in0=y2[:, j, :],
                                                    scalar=gates[:, 1, 4 * g + j:4 * g + j + 1],
                                                    in1=f0[:, j, :], op0=ALU.mult, op1=ALU.add)
                last.then_inc(t_f, 1)
                dve.wait_ge(t_f, g + 1)

            def wide(v):
                return v.rearrange("p (i n) -> p i n", i=2)

            def over(v):
                return v.rearrange("p (a n) -> p a n", a=1).broadcast_to([P, 2, 512])

            def rows_of(v):
                return v.rearrange("p (r d) -> p r d", d=D)

            def products(g):
                par = g % 2
                f, a, b, u1 = FV[par], PA[par], PB[par], U1[par]
                if g >= 2:
                    dve.wait_ge(t_mm, g - 1)
                dve.tensor_tensor(wide(a), over(A0), wide(f), ALU.mult)
                dve.tensor_tensor(wide(PR[par]), over(B1), wide(f), ALU.mult)
                link(dve.tensor_tensor(wide(b), over(gr[:, 2, :]), wide(f), ALU.mult))
                for kind in range(2):
                    for side in range(2):
                        for i in range(2):
                            fe = edge_cols(rows_of(f))[side][:, 2 * i:2 * i + 2, :]
                            last = dve.tensor_tensor(edge_p[:, par, kind, 2 * i:2 * i + 2, side, :], fe,
                                                     edge_w[:, kind, :, 4 * side:4 * side + 4], ALU.mult)
                bv, cv = rows_of(b), rows_of(CC[par])
                link(dve.tensor_tensor(cv[:, :, 1:D - 1], bv[:, :, 2:D], bv[:, :, 0:D - 2], ALU.subtract))
                link(dve.tensor_reduce(cv[:, :, 0:D:D - 1], edge_p[:, par, 1, :, :, :], AX_X, ALU.add))
                dve.tensor_tensor(u1, CC[par], a, ALU.subtract).then_inc(t_u1, 1)

            def column_terms(g):
                par = g % 2
                dve.wait_ge(t_q, g + 1)
                sv, pv, qv = rows_of(SM[par]), rows_of(PP[par]), rows_of(PQ[par])
                link(dve.tensor_tensor(sv[:, :, 1:D - 1], pv[:, :, 2:D], qv[:, :, 0:D - 2], ALU.add))
                link(dve.tensor_tensor(sv[:, :, 1:D - 1], sv[:, :, 1:D - 1], rows_of(PR[par])[:, :, 1:D - 1],
                                       ALU.subtract))
                dve.tensor_reduce(sv[:, :, 0:D:D - 1], edge_p[:, par, 0, :, :, :], AX_X, ALU.add).then_inc(t_sum, 1)
                dve.wait_ge(t_sum, g + 1)

            def update(g):
                par = g % 2
                dve.wait_ge(t_mm, g + 1)
                s4 = SM[par].rearrange("p (i q d) -> p i q d", i=2, q=2)
                for q in range(2):
                    last = dve.tensor_tensor(s4[:, :, q, :],
                                             banks[2 * par + q][:, :].rearrange("p (i d) -> p i d", i=2),
                                             s4[:, :, q, :], ALU.add)
                link(last)
                if g >= 2:
                    dve.wait_ge(t_relu, g - 1)
                for i in range(2):
                    b = 2 * g + i
                    at = slice(512 * i, 512 * i + 512)
                    last = dve.scalar_tensor_tensor(out=TT[par][:, at], in0=SM[par][:, at], scalar=dt_b[:, b:b + 1],
                                                    in1=FV[par][:, at], op0=ALU.mult, op1=ALU.add)
                last.then_inc(t_fin, 1)

            for g in range(NPAIR + 1):
                if g < NPAIR:
                    add_up(g)
                    products(g)
                if g >= 1:
                    update(g - 1)
                if g < NPAIR:
                    column_terms(g)


_INS = ['x', 'itok_B_6_14', 'condB_dt', 'L0_cond_exp_w1', 'L0_cond_exp_b1', 'L0_cond_exp_w2', 'L0_cond_exp_b2',
        'L1_cond_A_grid', 'L1_cond_B_grid']


def kernel(**inputs):
    import concourse.bacc as _bacc
    from concourse.bass_utils import run_bass_kernel_spmd as _run

    nc = _bacc.Bacc("TRN2", target_bir_lowering=False, num_devices=1)
    arrays, args = {}, []
    given = {name: np.ascontiguousarray(inputs[name]) for name in _INS}
    for name, a in {**given, "small": pack(inputs), "constants": constants()}.items():
        arrays[f"in_{name}_dram"] = a
        args.append(nc.dram_tensor(f"in_{name}_dram", a.shape, mybir.dt.from_np(a.dtype), kind="ExternalInput").ap())
    args.append(nc.dram_tensor("out_0_dram", (NB, T, D), F32, kind="ExternalOutput").ap())
    moe_then_stencil(nc, *args)
    r = _run(nc, [arrays], core_ids=[0])
    return r.results[0]["out_0_dram"]
```

```python
from contextlib import ExitStack

import numpy as np

import concourse.bass as bass
from concourse import mybir

ALU = mybir.AluOpType
ACT = mybir.ActivationFunctionType
F32 = mybir.dt.float32
F32R = mybir.dt.float32r
BF16 = mybir.dt.bfloat16
I32 = mybir.dt.int32
AX_X = mybir.AxisListType.X

P = 128
NB, T, D = 8, 256, 256
N = NB * T
NJ = N // P
KD = D // P
E, FF, TOPK = 8, 1024, 2
S_SUB, SE, SH = 32, 64, 128
FB = FF // P
ST = 256
TB = ST // P
NS = N * TOPK // ST + E - 1
NC = NS * TB
BANKS = FB // 2
EMPTY = 8192.0

C_IDENT = 0
C_PART = C_IDENT + P
C_BEFORE = C_PART + 2
C_EXPERT = C_BEFORE + P
C_SLOT = C_EXPERT + NJ * E
C_FRONT = C_SLOT + NS * E
C_D1 = C_FRONT
C_D2 = C_D1 + KD * T
C_EDGE = C_D2 + KD * T
C_ALL = C_EDGE + 24


def stencil(n):
    d1, d2 = np.zeros((n, n)), np.zeros((n, n))
    for i in range(1, n - 1):
        d1[i, i - 1], d1[i, i + 1] = -0.5, 0.5
        d2[i, i - 1], d2[i, i], d2[i, i + 1] = 1, -2, 1
    d1[0, :3] = [-1.5, 2, -0.5]
    d1[-1, -3:] = [0.5, -2, 1.5]
    d2[0, :4] = [2, -5, 4, -1]
    d2[-1, -4:] = [-1, 4, -5, 2]
    return d1, d2


def constants():
    c = np.zeros((P, C_ALL), np.float32)
    p = np.arange(P)
    c[:, C_IDENT:C_IDENT + P] = np.eye(P)
    c[:, C_BEFORE:C_BEFORE + P] = p[:, None] < p[None, :]
    c[:, C_EXPERT:C_EXPERT + NJ * E] = np.tile(np.arange(E), NJ)
    c[:, C_SLOT:C_SLOT + NS * E] = np.repeat(np.arange(NS), E)
    c[:, C_PART] = p
    c[:, C_PART + 1] = p + 1
    d1, d2 = stencil(T)
    c[:, C_D1:C_D1 + KD * T] = d1.T.reshape(KD, P, T).transpose(1, 0, 2).reshape(P, -1)
    c[:, C_D2:C_D2 + KD * T] = 0.5 * d2.T.reshape(KD, P, T).transpose(1, 0, 2).reshape(P, -1)
    for n, (m, w, own) in enumerate(((d2, 0.5, 1.0), (d1, -1.0, 0.0), (d1, 1.0, 0.0))):
        c[:, C_EDGE + 8 * n:C_EDGE + 8 * n + 4] = w * m[0, :4]
        c[:, C_EDGE + 8 * n + 4:C_EDGE + 8 * n + 8] = w * m[-1, -4:]
        c[:, C_EDGE + 8 * n] += own
        c[:, C_EDGE + 8 * n + 7] += own
    return c


SMALL = {}
for _name, _rows, _cols in (("ln_g", P, KD), ("ln_b", P, KD), ("router_w", P, KD * E), ("hyp_b1", SH, 1),
                            ("hyp_b2", SH, 1), ("sty_b1", SH // 2, 1), ("sty_b2", P, 2 * D // P),
                            ("subj_emb", S_SUB, SE), ("hyp_w1", SE, SH), ("hyp_w2", SH, SH),
                            ("sty_w1", SH, SH // 2), ("sty_w2", SH // 2, 2 * D)):
    SMALL[_name] = (_rows, _cols, sum(v[1] for v in SMALL.values()))
SMALL_ALL = sum(v[1] for v in SMALL.values())


def pack(inputs):
    out = np.zeros((P, SMALL_ALL), np.float32)
    for name, (rows, cols, at) in SMALL.items():
        a = np.asarray(inputs["L0_cond_" + name])
        if name == "router_w":
            a = a.reshape(KD, P, E).transpose(1, 0, 2)
        elif a.ndim == 1 and cols > 1:
            a = a.reshape(cols, P).T
        out[:rows, at:at + cols] = a.reshape(rows, cols)
    return out


def moe_then_stencil(nc, x, ids, dt, exp_w1, exp_b1, exp_w2, exp_b2, a_grid, b_grid, small, consts, out):
    h_rows = nc.dram_tensor("h_rows", (N, D), F32, kind="Internal").ap()
    y_rows = nc.dram_tensor("y_rows", (TOPK * N, D), F32, kind="Internal").ap()

    ctx = ExitStack()
    with ctx:
        def sb(name, shape, dt_=F32):
            return ctx.enter_context(nc.sbuf_tensor(name, shape, dt_))

        def sem(name):
            return ctx.enter_context(nc.semaphore(name))

        psum = ctx.enter_context(nc.psum_tensor("psum", [P, 8, 512], F32))
        banks = [psum[:, i, :] for i in range(8)]

        x_sb = sb("x_sb", [P, NJ, D])
        cst = sb("cst", [P, C_ALL])
        ident = cst[:, C_IDENT:C_IDENT + P]
        gates = sb("gates", [P, TOPK, NJ])
        mx = sb("mx", [P, TOPK, NJ])
        dst_i = sb("dst_i", [P, NC], I32)
        src_i = sb("src_i", [P, NC + TB], I32)
        e_idx = sb("e_idx", [1, NS], I32)
        ones8 = sb("ones8", [P, E])
        b2_all = sb("b2_all", [P, E, D])
        b1_all = sb("b1_all", [P, E, FB])
        grid = sb("grid", [P, 5, KD, D])
        gr = sb("gr", [P, 3, KD * D])
        dt_b = sb("dt_b", [P, NB])
        dt_n = sb("dt_n", [P, NB])
        edge_w = sb("edge_w", [P, 2, 2 * KD, 8])
        edge_t = sb("edge_t", [P, KD, 8])

        with ExitStack() as phase:
            def own(name, shape, dt_=F32):
                return phase.enter_context(nc.sbuf_tensor(name, shape, dt_))

            raw_a = own("raw_a", [P, 2, 2048])
            raw_b = own("raw_b", [P, 2, 2048])
            w_split = own("w_split", [P, 2, 2, 2, 2048], F32R)
            hid = own("hid", [P, 2, 2, FB, ST], F32R)
            relu = own("relu", [P, 2, 2, ST])
            slot_h = own("slot_h", [P, 2, 2, KD, ST], F32R)
            gathered = own("gathered", [P, 2, TB, D])
            y_sb = own("y_sb", [P, 2, TB, D])
            b1_cur = own("b1_cur", [P, 2, FB])
            src_cur = own("src_cur", [P, 2, TB], I32)
            dst_cur = own("dst_cur", [P, 2, TB], I32)
        w1_raw = [raw_a[:, i, :] for i in range(2)]
        w2_raw = [raw_b[:, i, :] for i in range(2)]

        with ExitStack() as phase:
            def own(name, shape, dt_=F32):
                return phase.enter_context(nc.sbuf_tensor(name, shape, dt_))

            h_pre = own("h_pre", [P, KD, N])
            hT = own("hT", [P, KD, N])
            own("w_split_first", [P, 10240])
            z = own("z", [P, 4, D])
            tok = own("tok", [P, 2, NC, TOPK * NJ], BF16)
            own("w_split_last", [P, 6144 - 1024 - TOPK * NJ * NC])
            h_tok = own("h_tok", [P, NJ, KD, P + E])
            oh_row = own("oh_row", [P, P, TOPK * NJ], BF16)
            oh_col = own("oh_col", [P, NC, TOPK * NJ], BF16)
            eye_rw = own("eye_rw", [P, KD, P + E])
            before_bf = own("before_bf", [P, P], BF16)
            ones_bf = own("ones_bf", [P, P], BF16)
            st1 = own("st1", [P, NJ, 6])
            mv1 = own("mv1", [P, NJ, 2])
            var1 = own("var1", [P, NJ])
            rs1 = own("rs1", [P, NJ])
            st2 = own("st2", [P, NB, KD, 6])
            mv2 = own("mv2", [P, NB, KD, 2])
            var2 = own("var2", [P, NB, KD])
            rs2 = own("rs2", [P, NB, KD])
            half = own("half", [P, 8])
            aff_a = own("aff_a", [P, NB, KD])
            aff_m = own("aff_m", [P, NB, KD])
            aff_b = own("aff_b", [P, NB, KD])
            id_i = own("id_i", [S_SUB, NB], I32)
            id_f = own("id_f", [S_SUB, NB])
            oh_s = own("oh_s", [S_SUB, NB])
            small_sb = own("small_sb", [P, SMALL_ALL])
            se_t = own("se_t", [SE, NB])
            hy1 = own("hy1", [SH, NB])
            hy2 = own("hy2", [SH, NB])
            sy1 = own("sy1", [SH // 2, NB])
            sty = own("sty", [P, 4, NB])
            gabs = own("gabs", [P, KD, NB])
            grelu = own("grelu", [P, KD, NB])
            gexp = own("gexp", [P, KD, NB])
            gln = own("gln", [P, KD, NB])
            gsum = own("gsum", [P, KD, NB])
            gam = own("gam", [P, KD, NB])
            lg = own("lg", [P, NJ, E])
            eq = own("eq", [P, NJ, E])
            cand = own("cand", [P, NJ, E])
            least = own("least", [P, NJ])
            oh = own("oh", [P, TOPK, NJ, E])
            lg2 = own("lg2", [P, NJ, E])
            gap = own("gap", [P, NJ])
            e2 = own("e2", [P, NJ])
            den = own("den", [P, NJ])
            m_bf = own("m_bf", [P, NJ, E], BF16)
            cnt_i = own("cnt_i", [P, E], I32)
            tl_i = own("tl_i", [P, E], I32)
            tl_f = own("tl_f", [P, E])
            t_end = own("t_end", [P, E])
            t_off = own("t_off", [P, E])
            base = own("base", [P, E])
            pos = own("pos", [P, NJ, E])
            pick = own("pick", [P, TOPK, NJ, E])
            slot_f = own("slot_f", [P, TOPK * NJ])
            slot_i = own("slot_i", [P, TOPK * NJ], I32)
            low_i = own("low_i", [P, TOPK * NJ], I32)
            col_i = own("col_i", [P, TOPK * NJ], I32)
            low_f = own("low_f", [P, TOPK * NJ], BF16)
            col_f = own("col_f", [P, TOPK * NJ], BF16)
            row_of = own("row_of", [P, P, TOPK * NJ], BF16)
            col_of = own("col_of", [P, NC, TOPK * NJ], BF16)
            tile_of = own("tile_of", [P, TOPK * NJ], BF16)
            e_cmp = own("e_cmp", [1, NS, E])
            e_sum = own("e_sum", [1, NS])
            num = own("num", [P, NC])
            num_e = own("num_e", [P, NC])
            num_f = own("num_f", [P, NC])

        def part(name):
            rows, cols, at = SMALL[name]
            return small_sb[0:rows, at:at + cols]

        rw_sb = part("router_w").rearrange("p (k e) -> p k e", k=KD)
        emb, hw1, hw2, sw1, sw2 = (part(n) for n in ("subj_emb", "hyp_w1", "hyp_w2", "sty_w1", "sty_w2"))
        hb1, hb2, sbi1, sbi2 = (part(n) for n in ("hyp_b1", "hyp_b2", "sty_b1", "sty_b2"))
        ln_gain, ln_offset = part("ln_g"), part("ln_b")

        with ExitStack() as phase:
            def own(name, shape, dt_=F32):
                return phase.enter_context(nc.sbuf_tensor(name, shape, dt_))

            Y1, Y2, F0, FV, FD, GG, GF, PA, PB, CC, U1, U2, PP, PQ, SM, TT, OUT = (
                [own(f"{n}_{par}", [P, 4 * D])[:, :] for par in range(2)]
                for n in ("t_y1", "t_y2", "t_f0", "t_f", "t_fd", "t_keep", "t_kept", "t_a0f", "t_b2f", "t_d1b2f",
                          "t_u1", "t_b0f", "t_pf", "t_qf", "t_cols", "t_new", "t_out"))
            edge_p = own("edge_p", [P, 2, 2, 4, 2, 4])

        x_in = [sem(f"x_in{i}") for i in range(4)]
        ident_in, cst_in = sem("ident_in"), sem("cst_in")
        sty_in = sem("sty_in")
        exp_in = sem("exp_in")
        grid_in = sem("grid_in")
        chain = sem("chain")
        half_set = sem("half_set")
        var1_ok = sem("var1_ok")
        rs1_ok = sem("rs1_ok")
        z_ok = sem("z_ok")
        fwd_t = sem("fwd_t")
        pre_ok = sem("pre_ok")
        var2_ok = sem("var2_ok")
        rs2_ok = sem("rs2_ok")
        aff_ok, ht_ok = sem("aff_ok"), sem("ht_ok")
        eye_ok, iota_ok = sem("eye_ok"), sem("iota_ok")
        back_t = sem("back_t")
        htok_ok = sem("htok_ok")
        hrows_out = sem("hrows_out")
        sty_pe = sem("sty_pe")
        sty_act = sem("sty_act")
        sty_dve = sem("sty_dve")
        gap_ok = sem("gap_ok")
        e2_ok = sem("e2_ok")
        m_ok = sem("m_ok")
        rank_ok = sem("rank_ok")
        tok_ok = sem("tok_ok")
        ohrow_ok = sem("ohrow_ok")
        perm_mm = sem("perm_mm")
        e_ok = sem("e_ok")
        w1_in = [sem(f"w1_in{i}") for i in range(2)]
        w2_in = [sem(f"w2_in{i}") for i in range(2)]
        w1_hi, w1_lo, w2_hi, w2_lo = sem("w1_hi"), sem("w1_lo"), sem("w2_hi"), sem("w2_lo")
        first_lo = sem("first_lo")
        h_hi, h_lo = sem("h_hi"), sem("h_lo")
        b1_ok = sem("b1_ok")
        l1_done, relu_ok, hid_hi, hid_lo, l2_done = (sem("l1_done"), sem("relu_ok"), sem("hid_hi"),
                                                     sem("hid_lo"), sem("l2_done"))
        pool_go = sem("pool_go")
        tr_done, y_ok = sem("tr_done"), sem("y_ok")
        src_ok, dst_ok = sem("src_ok"), sem("dst_ok")
        rows_in = [sem(f"rows_in{i}") for i in range(2)]
        y_out = [sem(f"y_out{i}") for i in range(2)]

        y_in = [sem(f"y_in{i}") for i in range(2)]
        t_f, t_u2, t_p, t_q = (sem(n) for n in ("t_f", "t_u2", "t_p", "t_q"))
        t_u1, t_mm, t_fin, t_relu = (sem(n) for n in ("t_u1", "t_mm", "t_fin", "t_relu"))
        t_keep, t_fd = sem("t_keep"), sem("t_fd")
        out_dma = [sem(f"out_dma{i}") for i in range(2)]
        grids_ok = sem("grids_ok")

        x_tok = x.rearrange("b (q p) d -> p (b q) d", p=P)
        out_tok = out.rearrange("b (q p) d -> p (b q) d", p=P)
        h_rows_tok = h_rows.rearrange("(j p) d -> p j d", p=P)
        y_rows_tok = y_rows.rearrange("(c j p) d -> c p j d", c=TOPK, p=P)
        w1_of = exp_w1.rearrange("e (k p) f -> p e k f", p=P)
        w2_of = exp_w2.rearrange("e (p b) d -> p e (b d)", b=FB)

        block = ctx.enter_context(nc.Block())

        NPAIR = NB // 2
        LOOP = range(1, (NS - 1) // 2)
        assert NS % 2 == 1

        @block.sync
        def _(sp):
            for i in range(4):
                sp.dma_start(x_sb[:, 4 * i:4 * i + 4, :], x_tok[:, 4 * i:4 * i + 4, :]).then_inc(x_in[i], 16)
            for b in range(NB):
                sp.wait_ge(htok_ok, b + 1)
                for j in range(2 * b, 2 * b + 2):
                    sp.dma_start(h_rows_tok[:, j, :].rearrange("p (k n) -> p k n", k=KD),
                                 h_tok[:, j, :, 0:P]).then_inc(hrows_out, 16)

            def weights(s, par, ring):
                e = sp.value_load(e_idx[0:1, bass.DynSlice(s, 1)], min_val=0, max_val=E - 1)
                if ring:
                    sp.wait_ge(w1_hi, s - 1)
                    sp.wait_ge(w1_lo, s - 1)
                sp.dma_start(w1_raw[par].rearrange("p (k f) -> p k f", k=KD),
                             w1_of[:, bass.DynSlice(e, 1), :, :].rearrange("p e k f -> p (e k) f")
                             ).then_inc(w1_in[par], 16)
                if ring:
                    sp.wait_ge(w2_hi, s - 1)
                    sp.wait_ge(w2_lo, s - 1)
                sp.dma_start(w2_raw[par], w2_of[:, bass.DynSlice(e, 1), :].rearrange("p e n -> p (e n)")
                             ).then_inc(w2_in[par], 16)

            sp.wait_ge(e_ok, 1)
            sp.wait_ge(back_t, NB)
            weights(0, 0, False)
            weights(1, 1, False)
            with sp.Fori(1, LOOP.stop) as m:
                for par in range(2):
                    weights(2 * m + par, par, True)
            weights(NS - 1, 0, True)

            sp.wait_ge(l2_done, NS)
            for par in range(2):
                sp.wait_ge(y_out[par], 32 * ((NS + 1 - par) // 2))
            for g in range(NPAIR):
                if g >= 2:
                    sp.wait_ge(t_f, g - 1)
                for c, buf in enumerate((Y1, Y2)):
                    sp.dma_start(buf[g % 2].rearrange("p (j d) -> p j d", j=4),
                                 y_rows_tok[c, :, 4 * g:4 * g + 4, :]).then_inc(y_in[g % 2], 16)
            for g in range(NPAIR):
                sp.wait_ge(t_relu, g + 1)
                sp.dma_start(out_tok[:, 4 * g:4 * g + 4, :],
                             OUT[g % 2].rearrange("p (j d) -> p j d", j=4)).then_inc(out_dma[g % 2], 16)
            for par in range(2):
                sp.wait_ge(out_dma[par], 16 * (NPAIR // 2))
            sp.wait_ge(hrows_out, 16 * NJ)

        @block.scalar
        def _(act):
            def load(dst, src, s):
                act.dma_start(dst, src).then_inc(s, 16)

            load(id_i[:, :], ids.rearrange("(a b) -> a b", a=1).partition_broadcast(S_SUB), sty_in)
            load(small_sb[:, :], small, sty_in)
            load(cst[:, 0:C_BEFORE], consts[:, 0:C_BEFORE], ident_in)
            load(cst[:, C_BEFORE:C_FRONT], consts[:, C_BEFORE:C_FRONT], cst_in)

            act.wait_ge(sty_in, 32)
            act.wait_ge(sty_pe, 1)
            act.activation(se_t[:, :], banks[1][0:SE, 0:NB], ACT.Copy).then_inc(sty_act, 1)
            act.wait_ge(sty_pe, 2)
            act.activation(hy1[:, :], banks[1][:, 8:8 + NB], ACT.Relu, bias=hb1[:, 0:1]).then_inc(sty_act, 1)
            act.wait_ge(sty_pe, 3)
            act.activation(hy2[:, :], banks[1][:, 16:16 + NB], ACT.Identity, bias=hb2[:, 0:1]).then_inc(sty_act, 1)
            act.wait_ge(sty_pe, 4)
            act.activation(sy1[:, :], banks[1][0:SH // 2, 24:24 + NB], ACT.Relu,
                           bias=sbi1[:, 0:1]).then_inc(sty_act, 1)
            act.wait_ge(sty_pe, 5)
            for c in range(4):
                last = act.activation(sty[:, c, :], banks[1][:, 32 + 8 * c:40 + 8 * c], ACT.Identity,
                                      bias=sbi2[:, c:c + 1])
            last.then_inc(sty_act, 1)
            def front(b):
                act.wait_ge(fwd_t, b + 1)
                for k in range(KD):
                    last = act.activation(h_pre[:, k, T * b:T * b + T], banks[4 + b % 2][:, T * k:T * k + T],
                                          ACT.Identity, bias=ln_offset[:, k:k + 1], scale=ln_gain[:, k:k + 1])
                last.then_inc(pre_ok, 1)

            def styled(b):
                act.wait_ge(aff_ok, b + 1)
                for k in range(KD):
                    last = act.activation(hT[:, k, T * b:T * b + T], h_pre[:, k, T * b:T * b + T], ACT.Identity,
                                          bias=aff_b[:, b, k:k + 1], scale=aff_a[:, b, k:k + 1])
                last.then_inc(ht_ok, 1)

            def rows(b):
                act.wait_ge(back_t, b + 1)
                at = 6 if b % 2 == 0 else 2
                act.activation(h_tok[:, 2 * b:2 * b + 2, :, :],
                               psum[:, at:at + 2, 0:KD * (P + E)].rearrange("p j (k n) -> p j k n", k=KD),
                               ACT.Copy).then_inc(htok_ok, 1)

            for i in range(NB + 4):
                if 3 <= i < NB + 3:
                    styled(i - 3)
                if i < NB:
                    front(i)
                if i == 1:
                    act.wait_ge(sty_act, 5)
                    act.activation(gabs[:, :, :], sty[:, 0:KD, :], ACT.Abs).then_inc(sty_act, 1)
                    act.wait_ge(sty_act, 6)
                    act.activation(gexp[:, :, :], gabs[:, :, :], ACT.Exp, scale=-1.0).then_inc(sty_act, 1)
                    act.wait_ge(sty_act, 7)
                    act.activation(gln[:, :, :], gexp[:, :, :], ACT.Ln, bias=ones8[:, 0:1]).then_inc(sty_act, 1)
                if i >= 4:
                    rows(i - 4)
                if i == 4:
                    load(cst[:, C_FRONT:C_ALL], consts[:, C_FRONT:C_ALL], grid_in)
                    load(b1_all[:, :, :], exp_b1.rearrange("e (p b) -> p e b", b=FB), exp_in)
                    load(b2_all[:, :, :], exp_b2.rearrange("(a e) d -> a e d", a=1).partition_broadcast(P), exp_in)
                    load(grid[:, 0:2, :, :], a_grid.rearrange("g (q p) d -> p g q d", p=P), grid_in)
                    load(grid[:, 2:5, :, :], b_grid.rearrange("g (q p) d -> p g q d", p=P), grid_in)
                    load(dt_b[:, :], dt.rearrange("(a b) -> a b", a=1).partition_broadcast(P), grid_in)

            act.wait_ge(gap_ok, 1)
            act.activation(e2[:, :], gap[:, :], ACT.Exp).then_inc(e2_ok, 1)

            def split_w1(s, par, landed, first=False):
                act.wait_ge(w1_in[par], landed)
                if not first:
                    act.wait_ge(l1_done, BANKS * (s - 1))
                act.activation(w_split[:, 0, par, 0, :].rearrange("p (k b f) -> p k b f", k=KD, b=FB),
                               w1_raw[par].rearrange("p (k f b) -> p k b f", k=KD, b=FB),
                               ACT.Copy).then_inc(w1_hi, 1)

            def split_w2(s, par, landed, first=False):
                act.wait_ge(w2_in[par], landed)
                if not first:
                    act.wait_ge(l2_done, s - 1)
                act.activation(w_split[:, 1, par, 0, :], w2_raw[par], ACT.Copy).then_inc(w2_hi, 1)

            def split_h(s, par, first=False, bank=6):
                act.wait_ge(tr_done, s + 1)
                if not first:
                    act.wait_ge(l1_done, BANKS * (s - 1))
                act.activation(slot_h[:, par, 0, :, :], banks[bank].rearrange("p (k n) -> p k n", k=KD),
                               ACT.Copy).then_inc(h_hi, 1)

            def step(s, par, landed, begin=BANKS, last_slot=False):
                e = act.value_load(e_idx[0:1, bass.DynSlice(s, 1)], min_val=0, max_val=E - 1)
                act.activation(b1_cur[:, par, :],
                               b1_all[:, bass.DynSlice(e, 1), :].rearrange("p e b -> p (e b)"),
                               ACT.Copy).then_inc(b1_ok, 1)
                act.wait_ge(b1_ok, s + 1)
                if not last_slot:
                    split_w1(s + 1, 1 - par, landed + 16 * par, first=begin == 0)
                for bank in range(BANKS):
                    act.wait_ge(l1_done, BANKS * s + bank + 1)
                    if begin > 0 or bank >= 2:
                        act.wait_ge(hid_lo, BANKS * s + bank - 1)
                    for i in range(2):
                        blk = 2 * bank + i
                        last = act.activation(relu[:, bank % 2, i, :], banks[bank][:, ST * i:ST * i + ST],
                                              ACT.Relu, bias=b1_cur[:, par, blk:blk + 1])
                    last.then_inc(relu_ok, 1)
                if not last_slot and begin > 0:
                    split_h(s + 1, 1 - par)
                split_w2(s, par, landed, first=begin < 2)

            act.wait_ge(exp_in, 32)
            act.wait_ge(e_ok, 1)
            split_w1(0, 0, 16, first=True)
            split_h(0, 0, first=True)
            split_h(1, 1, first=True, bank=7)
            step(0, 0, 16, begin=0)
            step(1, 1, 16, begin=1)
            with act.Fori(1, LOOP.stop) as m:
                for par in range(2):
                    step(2 * m + par, par, 16 * m + 16)
            step(NS - 1, 0, 16 * ((NS - 1) // 2) + 16, last_slot=True)

            def relu_out(g):
                act.wait_ge(t_fin, g + 1)
                if g >= 2:
                    act.wait_ge(out_dma[g % 2], 16 * (g // 2))
                act.activation(OUT[g % 2], TT[g % 2], ACT.Relu).then_inc(t_relu, 1)

            act.wait_ge(grids_ok, 1)
            act.wait_ge(l2_done, NS)
            act.wait_ge(y_ok, NS)
            for g in range(NPAIR):
                par = g % 2
                if g >= 2:
                    act.wait_ge(t_u1, g - 1)
                    act.wait_ge(t_q, g - 1)
                for i in range(2):
                    last = act.activation(GG[par][:, 512 * i:512 * i + 512],
                                          grid[:, 3, :, :].rearrange("p q d -> p (q d)"), ACT.Identity,
                                          bias=ones8[:, 0:1], scale=dt_n[:, 2 * g + i:2 * g + i + 1])
                last.then_inc(t_keep, 1)
                act.wait_ge(t_f, g + 1)
                for i in range(2):
                    last = act.activation(FD[par][:, 512 * i:512 * i + 512], FV[par][:, 512 * i:512 * i + 512],
                                          ACT.Copy, scale=dt_b[:, 2 * g + i:2 * g + i + 1])
                last.then_inc(t_fd, 1)
                if g >= 1:
                    relu_out(g - 1)
            relu_out(NPAIR - 1)

        @block.gpsimd
        def _(pool):
            pool.memset(half[:, :], -0.5).then_inc(half_set, 1)
            pool.wait_ge(half_set, 1)

            def number(out, pattern):
                pool.iota(out, pattern=pattern, base=0, channel_multiplier=0,
                          allow_small_or_imprecise_dtypes=True).then_inc(iota_ok, 1)

            for i in range(NB + 3):
                if i < NB:
                    pool.wait_ge(var1_ok, i + 1)
                    pool.tensor_tensor(rs1[:, 2 * i:2 * i + 2], var1[:, 2 * i:2 * i + 2], half[:, 0:2],
                                       ALU.pow).then_inc(rs1_ok, 1)
                if i == 0:
                    number(tile_of[:, :], [[1, TOPK * NJ]])
                    number(col_of[:, :, :], [[1, NC], [0, TOPK * NJ]])
                if i == NB:
                    number(row_of[:, :, :], [[1, P], [0, TOPK * NJ]])
                if i >= 3:
                    pool.wait_ge(var2_ok, i - 2)
                    pool.tensor_tensor(rs2[:, i - 3, :], var2[:, i - 3, :], half[:, 0:KD],
                                       ALU.pow).then_inc(rs2_ok, 1)

            def gather(s, par, ring):
                pool.wait_ge(src_ok, s + 1)
                if ring:
                    pool.wait_ge(tr_done, s - 1)
                pool.sem_inc(pool_go, 1)
                for t in range(TB):
                    pool.indirect_dma_start(
                        out=gathered[:, par, t, :], out_offset=None, in_=h_rows,
                        in_offset=bass.IndirectOffsetOnAxis(ap=src_cur[:, par, t:t + 1], axis=0),
                    ).then_inc(rows_in[par], 16)

            def scatter(s, par):
                pool.wait_ge(y_ok, s + 1)
                pool.wait_ge(dst_ok, s + 1)
                pool.sem_inc(pool_go, 1)
                for t in range(TB):
                    pool.indirect_dma_start(
                        out=y_rows, out_offset=bass.IndirectOffsetOnAxis(ap=dst_cur[:, par, t:t + 1], axis=0),
                        in_=y_sb[:, par, t, :], in_offset=None, bounds_check=TOPK * N - 1, oob_is_err=False,
                    ).then_inc(y_out[par], 16)

            def high(s, par, ring):
                for bank in range(BANKS):
                    pool.wait_ge(relu_ok, BANKS * s + bank + 1)
                    if ring and bank == 0:
                        pool.wait_ge(l2_done, s - 1)
                    pool.sem_inc(pool_go, 1)
                    pool.tensor_scalar(hid[:, par, 0, 2 * bank:2 * bank + 2, :], relu[:, bank % 2, :, :],
                                       1.0, 0.0, ALU.mult, ALU.add).then_inc(hid_hi, 1)

            pool.wait_ge(w1_hi, 1)
            pool.tensor_tensor(w_split[:, 0, 0, 1, :].rearrange("p (k b f) -> p k b f", k=KD, b=FB),
                               w1_raw[0].rearrange("p (k f b) -> p k b f", k=KD, b=FB),
                               w_split[:, 0, 0, 0, :].rearrange("p (k b f) -> p k b f", k=KD, b=FB).bitcast(F32),
                               ALU.subtract).then_inc(first_lo, 1)
            pool.wait_ge(hrows_out, 16 * NJ)
            gather(0, 0, False)
            gather(1, 1, False)
            for s in range(2):
                gather(s + 2, s, True)
                high(s, s, False)
            with pool.Fori(1, LOOP.stop) as m:
                for par in range(2):
                    s = 2 * m + par
                    gather(s + 2, par, True)
                    high(s, par, True)
                    scatter(s - 2, par)
            high(NS - 1, 0, True)
            scatter(NS - 3, 0)
            scatter(NS - 2, 1)
            scatter(NS - 1, 0)

            for g in range(NPAIR):
                par = g % 2
                f = FD[par].rearrange("p (i n) -> p i n", i=2)
                pool.wait_ge(t_fd, g + 1)
                if g >= 2:
                    pool.wait_ge(t_mm, g - 1)
                    pool.wait_ge(t_fin, g - 1)
                jobs = [(U2, grid[:, 2:3, :, :].rearrange("p a q d -> p a (q d)"), t_u2)]
                if g < NPAIR - 1:
                    jobs += [(PP, gr[:, 0:1, :], t_p), (PQ, gr[:, 1:2, :], t_q)]
                for dst, by, done in jobs:
                    pool.tensor_tensor(dst[par].rearrange("p (i n) -> p i n", i=2), by.broadcast_to([P, 2, 512]), f,
                                       ALU.mult).then_inc(done, 1)

        @block.tensor
        def _(pe):
            pe.wait_ge(sty_in, 32)
            pe.wait_ge(sty_dve, 1)
            pe.matmul(banks[1][0:SE, 0:NB], emb[:, :], oh_s[:, :], start=True, stop=True).then_inc(sty_pe, 1)
            pe.wait_ge(sty_act, 1)
            pe.matmul(banks[1][:, 8:8 + NB], hw1[:, :], se_t[:, :], start=True, stop=True).then_inc(sty_pe, 1)
            pe.wait_ge(sty_act, 2)
            pe.matmul(banks[1][:, 16:16 + NB], hw2[:, :], hy1[:, :], start=True, stop=True).then_inc(sty_pe, 1)
            pe.wait_ge(sty_act, 3)
            pe.matmul(banks[1][0:SH // 2, 24:24 + NB], sw1[:, :], hy2[:, :], start=True, stop=True).then_inc(sty_pe, 1)
            pe.wait_ge(sty_act, 4)
            for c in range(4):
                last = pe.matmul(banks[1][:, 32 + 8 * c:40 + 8 * c], sw2[:, P * c:P * c + P], sy1[:, :],
                                 start=True, stop=True)
            last.then_inc(sty_pe, 1)

            pe.wait_ge(ident_in, 16)

            def forward(b):
                pe.wait_ge(z_ok, b + 1)
                if b >= 2:
                    pe.wait_ge(pre_ok, b - 1)
                for k in range(KD):
                    for q in range(2):
                        last = pe.transpose(banks[4 + b % 2][:, T * k + P * q:T * k + P * q + P],
                                            z[:, (2 * b + q) % 4, P * k:P * k + P], ident)
                last.then_inc(fwd_t, 1)

            def back(b):
                pe.wait_ge(ht_ok, b + 1)
                if b >= 2:
                    pe.wait_ge(htok_ok, b - 1)
                for q in range(2):
                    for k in range(KD):
                        at = (P + E) * k
                        last = pe.matmul(banks[(6 if b % 2 == 0 else 2) + q][:, at:at + P + E],
                                         hT[:, k, T * b + P * q:T * b + P * q + P], eye_rw[:, k, :],
                                         start=True, stop=True)
                last.then_inc(back_t, 1)

            for i in range(NB + 3):
                if i < NB:
                    forward(i)
                if i == 3:
                    pe.wait_ge(eye_ok, 1)
                if i >= 3:
                    back(i - 3)

            pe.wait_ge(m_ok, 1)
            rank = banks[2][:, 0:NJ * E]
            pe.matmul(rank, before_bf[:, :], m_bf[:, :, :].rearrange("p j e -> p (j e)"), start=True, stop=False)
            for d in range(1, NJ):
                pe.matmul(rank[:, E * d:NJ * E], ones_bf[:, :],
                          m_bf[:, 0:NJ - d, :].rearrange("p j e -> p (j e)"), start=False, stop=(d == NJ - 1))
            for j in range(NJ):
                last = pe.matmul(banks[3][:, 0:E], ones_bf[:, :], m_bf[:, j, :], start=(j == 0), stop=(j == NJ - 1))
            last.then_inc(rank_ok, 1)

            pe.wait_ge(tok_ok, 1)
            for t in range(TOPK * NJ):
                if t % NJ == 0:
                    pe.wait_ge(ohrow_ok, t // NJ + 1)
                last = pe.matmul(banks[1][:, 128:128 + 2 * NC], oh_row[:, :, t],
                                 tok[:, :, :, t].rearrange("p a n -> p (a n)"),
                                 start=(t == 0), stop=(t == TOPK * NJ - 1))
            last.then_inc(perm_mm, 1)

            def turn(s, par, mr, first=False, bank=6):
                pe.wait_ge(rows_in[par], mr)
                if not first:
                    pe.wait_ge(h_hi, s)
                    pe.wait_ge(h_lo, s)
                for k in range(KD):
                    for t in range(TB):
                        last = pe.transpose(banks[bank][:, ST * k + P * t:ST * k + P * t + P],
                                            gathered[:, par, t, P * k:P * k + P], ident)
                last.then_inc(tr_done, 1)

            PARTS = ((0, 0), (0, 1), (1, 0))

            def layer1(s, par, first=False):
                pe.wait_ge(w1_hi, s + 1)
                pe.wait_ge(w1_lo, s + 1)
                pe.wait_ge(h_hi, s + 1)
                pe.wait_ge(h_lo, s + 1)
                for blk in range(FB):
                    bank = blk // 2
                    if blk % 2 == 0 and not first:
                        pe.wait_ge(relu_ok, BANKS * s + bank - 3)
                    n = 0
                    for k in range(KD):
                        for w, h in PARTS:
                            at = (k * FB + blk) * P
                            last = pe.matmul(banks[bank][:, ST * (blk % 2):ST * (blk % 2) + ST],
                                             w_split[:, 0, par, w, at:at + P], slot_h[:, par, h, k, :],
                                             start=(n == 0), stop=(n == 3 * KD - 1))
                            n += 1
                    if blk % 2:
                        last.then_inc(l1_done, 1)

            def layer2(s, par, ring):
                pe.wait_ge(w2_hi, s + 1)
                pe.wait_ge(w2_lo, s + 1)
                pe.wait_ge(hid_lo, BANKS * (s + 1))
                if ring:
                    pe.wait_ge(y_ok, s - 1)
                for t in range(TB):
                    n = 0
                    for blk in range(FB):
                        for h, w in PARTS:
                            last = pe.matmul(banks[4 + par][:, D * t:D * t + D],
                                             hid[:, par, h, blk, P * t:P * t + P],
                                             w_split[:, 1, par, w, D * blk:D * blk + D],
                                             start=(n == 0), stop=(n == 3 * FB - 1))
                            n += 1
                last.then_inc(l2_done, 1)

            turn(0, 0, 32, first=True)
            turn(1, 1, 32, first=True, bank=7)
            layer1(0, 0, first=True)
            layer1(1, 1)
            turn(2, 0, 64)
            layer2(0, 0, False)
            layer1(2, 0)
            turn(3, 1, 64)
            layer2(1, 1, False)
            with pe.Fori(1, LOOP.stop) as m:
                layer1(2 * m + 1, 1)
                turn(2 * m + 2, 0, 32 * m + 64)
                layer2(2 * m, 0, True)
                layer1(2 * m + 2, 0)
                turn(2 * m + 3, 1, 32 * m + 64)
                layer2(2 * m + 1, 1, True)
            layer2(NS - 1, 0, True)

            for g in range(NPAIR):
                pe.wait_ge(t_u1, g + 1)
                pe.wait_ge(t_u2, g + 1)
                if g >= 2:
                    pe.wait_ge(t_fin, g - 1)
                for q in range(2):
                    n = 0
                    kept = GF[g % 2].rearrange("p (i q d) -> p q i d", i=2, q=2)
                    pe.matmul(banks[2 * (g % 2) + q].rearrange("p (i d) -> p i d", i=2), ident, kept[:, q, :, :],
                              start=True, stop=False)
                    for col, u in ((C_D1, U1[g % 2]), (C_D2, U2[g % 2])):
                        uv = u.rearrange("p (i q d) -> p q i d", i=2, q=2)
                        for k in range(2):
                            last = pe.matmul(banks[2 * (g % 2) + q].rearrange("p (i d) -> p i d", i=2),
                                             cst[:, col + T * k + P * q:col + T * k + P * q + P], uv[:, k, :, :],
                                             start=False, stop=(n == 3))
                            n += 1
                last.then_inc(t_mm, 1)

        @block.vector
        def _(dve):
            steps = [0]

            def link(ins):
                steps[0] += 1
                ins.then_inc(chain, 1)
                dve.wait_ge(chain, steps[0])

            link(dve.memset(ones8[:, :], 1.0))

            def front(i):
                chan, aff = i - 3, i - 4
                do_tok, do_chan, do_aff = i < NB, 0 <= chan < NB, aff >= 0
                if do_tok:
                    if i % 2 == 0:
                        dve.wait_ge(x_in[i // 2], 16)
                    for j in range(2 * i, 2 * i + 2):
                        last = dve.bn_stats(st1[:, j, :], x_sb[:, j, :])
                b = i - 1
                if 0 <= b < NB:
                    dve.wait_ge(rs1_ok, b + 1)
                    if b >= 2:
                        dve.wait_ge(fwd_t, b - 1)
                    for j in range(2 * b, 2 * b + 2):
                        norm = dve.tensor_scalar(z[:, j % 4, :], x_sb[:, j, :], mv1[:, j, 0:1], rs1[:, j:j + 1],
                                                 ALU.subtract, ALU.mult)
                    norm.then_inc(z_ok, 1)
                if do_aff:
                    dve.wait_ge(rs2_ok, aff + 1)
                    last = dve.tensor_tensor(aff_a[:, aff, :], rs2[:, aff, :], gam[:, :, aff], ALU.mult)
                if do_chan:
                    dve.wait_ge(pre_ok, chan + 1)
                    for k in range(KD):
                        last = dve.bn_stats(st2[:, chan, k, :], h_pre[:, k, T * chan:T * chan + T])
                if not (do_tok or do_aff or do_chan):
                    return
                link(last)
                if do_tok:
                    for j in range(2 * i, 2 * i + 2):
                        last = dve.bn_aggr(mv1[:, j, :], st1[:, j, :])
                if do_aff:
                    last = dve.tensor_tensor(aff_m[:, aff, :], mv2[:, aff, :, 0], aff_a[:, aff, :], ALU.mult)
                if do_chan:
                    for k in range(KD):
                        last = dve.bn_aggr(mv2[:, chan, k, :], st2[:, chan, k, :])
                link(last)
                if do_tok:
                    dve.tensor_scalar(var1[:, 2 * i:2 * i + 2], mv1[:, 2 * i:2 * i + 2, 1], 1e-5, None,
                                      ALU.add).then_inc(var1_ok, 1)
                if do_chan:
                    dve.tensor_scalar(var2[:, chan, :], mv2[:, chan, :, 1], 1e-8, None, ALU.add).then_inc(var2_ok, 1)
                if do_aff:
                    dve.tensor_tensor(aff_b[:, aff, :], sty[:, KD:2 * KD, aff], aff_m[:, aff, :],
                                      ALU.subtract).then_inc(aff_ok, 1)

            for i in range(NB + 4):
                if i == 0:
                    dve.wait_ge(sty_in, 32)
                    dve.wait_ge(ident_in, 16)
                    link(dve.tensor_copy(id_f[:, :], id_i[:, :]))
                    dve.tensor_scalar(oh_s[:, :], id_f[:, :], cst[0:S_SUB, C_PART:C_PART + 1], None,
                                      ALU.is_equal).then_inc(sty_dve, 1)
                if i == 2:
                    for k in range(KD):
                        dve.tensor_copy(eye_rw[:, k, 0:P], ident)
                    dve.tensor_copy(eye_rw[:, :, P:P + E], rw_sb).then_inc(eye_ok, 1)
                if i == 4:
                    dve.wait_ge(sty_act, 8)
                    link(dve.tensor_scalar(grelu[:, :, :], sty[:, 0:KD, :], 0.0, None, ALU.max))
                    link(dve.tensor_tensor(gsum[:, :, :], grelu[:, :, :], gln[:, :, :], ALU.add))
                    link(dve.tensor_scalar(gam[:, :, :], gsum[:, :, :], 1e-8, None, ALU.add))
                if i == NB:
                    dve.wait_ge(cst_in, 16)
                    dve.memset(ones_bf[:, :], 1.0)
                    dve.tensor_copy(before_bf[:, :], cst[:, C_BEFORE:C_BEFORE + P])
                front(i)

            dve.wait_ge(htok_ok, NB)
            link(dve.tensor_tensor(lg[:, :, :], h_tok[:, :, 0, P:P + E], h_tok[:, :, 1, P:P + E], ALU.add))
            expert = cst[:, C_EXPERT:C_EXPERT + NJ * E].rearrange("p (j e) -> p j e", e=E)

            def spread(v):
                return v.rearrange("p (j a) -> p j a", a=1).broadcast_to([P, NJ, E])

            for c, src in enumerate((lg, lg2)):
                link(dve.tensor_reduce(mx[:, c, :], src[:, :, :], AX_X, ALU.max))
                link(dve.tensor_tensor(eq[:, :, :], src[:, :, :], spread(mx[:, c, :]), ALU.is_equal))
                link(dve.scalar_tensor_tensor(out=cand[:, :, :], in0=eq[:, :, :], scalar=-2.0 * E, in1=expert,
                                              op0=ALU.mult, op1=ALU.add))
                link(dve.tensor_reduce(least[:, :], cand[:, :, :], AX_X, ALU.min))
                link(dve.tensor_tensor(oh[:, c, :, :], cand[:, :, :], spread(least[:, :]), ALU.is_equal))
                if c == 0:
                    link(dve.scalar_tensor_tensor(out=lg2[:, :, :], in0=oh[:, 0, :, :], scalar=-3e38,
                                                  in1=lg[:, :, :], op0=ALU.mult, op1=ALU.add))
            dve.tensor_tensor(gap[:, :], mx[:, 1, :], mx[:, 0, :], ALU.subtract).then_inc(gap_ok, 1)
            dve.tensor_tensor(m_bf[:, :, :], oh[:, 0, :, :], oh[:, 1, :, :], ALU.add).then_inc(m_ok, 1)

            dve.wait_ge(e2_ok, 1)
            link(dve.tensor_scalar(den[:, :], e2[:, :], 1.0, None, ALU.add))
            link(dve.reciprocal(gates[:, 0, :], den[:, :]))
            link(dve.tensor_tensor(gates[:, 1, :], e2[:, :], gates[:, 0, :], ALU.mult))

            dve.wait_ge(rank_ok, 1)
            link(dve.tensor_scalar(cnt_i[:, :], banks[3][:, 0:E], float(ST - 1), None, ALU.add))
            link(dve.tensor_scalar(tl_i[:, :], cnt_i[:, :], ST.bit_length() - 1, None, ALU.arith_shift_right))
            link(dve.tensor_copy(tl_f[:, :], tl_i[:, :]))
            link(dve.tensor_tensor_scan(t_end[:, :], ones8[:, :], tl_f[:, :], 0.0, ALU.mult, ALU.add))
            link(dve.tensor_tensor(t_off[:, :], t_end[:, :], tl_f[:, :], ALU.subtract))
            link(dve.tensor_tensor(e_cmp[:, :, :],
                                   t_off[0:1, :].rearrange("p (a e) -> p a e", a=1).broadcast_to([1, NS, E]),
                                   cst[0:1, C_SLOT:C_SLOT + NS * E].rearrange("p (s e) -> p s e", e=E), ALU.is_le))
            link(dve.tensor_reduce(e_sum[:, :], e_cmp[:, :, :], AX_X, ALU.add))
            dve.tensor_scalar(e_idx[:, :], e_sum[:, :], -1.0, None, ALU.add).then_inc(e_ok, 1)
            link(dve.tensor_scalar(base[:, :], t_off[:, :], float(ST), None, ALU.mult))
            link(dve.tensor_tensor(pos[:, :, :], banks[2][:, 0:NJ * E].rearrange("p (j e) -> p j e", e=E),
                                   base[:, :].rearrange("p (a e) -> p a e", a=1).broadcast_to([P, NJ, E]), ALU.add))
            link(dve.tensor_tensor(
                pick[:, :, :, :].rearrange("p c j e -> p c (j e)"), oh[:, :, :, :].rearrange("p c j e -> p c (j e)"),
                pos[:, :, :].rearrange("p (a j) e -> p a (j e)", a=1).broadcast_to([P, TOPK, NJ * E]), ALU.mult))
            link(dve.tensor_reduce(slot_f[:, :], pick[:, :, :, :].rearrange("p c j e -> p (c j) e"), AX_X, ALU.add))
            link(dve.tensor_copy(slot_i[:, :], slot_f[:, :]))
            dve.tensor_scalar(col_i[:, :], slot_i[:, :], P.bit_length() - 1, None, ALU.arith_shift_right)
            link(dve.tensor_scalar(low_i[:, :], slot_i[:, :], P - 1, None, ALU.bitwise_and))
            dve.tensor_copy(col_f[:, :], col_i[:, :])
            link(dve.tensor_copy(low_f[:, :], low_i[:, :]))
            TC = TOPK * NJ

            def by_tile(v, n):
                return v.rearrange("p (a t) -> p a t", a=1).broadcast_to([P, n, TC])

            dve.wait_ge(iota_ok, 3)
            link(dve.tensor_tensor(oh_col[:, :, :], by_tile(col_f[:, :], NC), col_of[:, :, :], ALU.is_equal))
            dve.tensor_scalar(tok[:, 0, :, :], oh_col[:, :, :], cst[:, C_PART + 1:C_PART + 2], None, ALU.mult)
            dve.tensor_tensor(tok[:, 1, :, :], oh_col[:, :, :], by_tile(tile_of[:, :], NC),
                              ALU.mult).then_inc(tok_ok, 1)
            for n in range(2):
                at = slice(NJ * n, NJ * n + NJ)
                dve.tensor_tensor(
                    oh_row[:, :, at],
                    low_f[:, at].rearrange("p (a t) -> p a t", a=1).broadcast_to([P, P, NJ]), row_of[:, :, at],
                    ALU.is_equal).then_inc(ohrow_ok, 1)
            dve.wait_ge(perm_mm, 1)
            parts = banks[1][:, 128:128 + 2 * NC]
            link(dve.tensor_copy(num_e[:, :], parts[:, 0:NC]))
            link(dve.scalar_tensor_tensor(out=num[:, :], in0=parts[:, NC:2 * NC], scalar=float(P), in1=num_e[:, :],
                                          op0=ALU.mult, op1=ALU.add))
            link(dve.tensor_scalar(num_f[:, :], num[:, :], 0.0, EMPTY, ALU.is_equal, ALU.mult))
            link(dve.scalar_tensor_tensor(out=dst_i[:, :], in0=num[:, :], scalar=-1.0, in1=num_f[:, :],
                                          op0=ALU.add, op1=ALU.add))
            dve.memset(src_i[:, NC:NC + TB], 0)
            link(dve.tensor_scalar(src_i[:, 0:NC], dst_i[:, :], N - 1, None, ALU.bitwise_and))

            def source(s, par, ring):
                if ring is not None:
                    dve.wait_ge(rows_in[par], ring)
                dve.tensor_copy(src_cur[:, par, :], src_i[:, bass.DynSlice(TB * s, TB)]).then_inc(src_ok, 1)

            def low_w1(s, par):
                dve.wait_ge(w1_hi, s + 1)
                dve.tensor_tensor(w_split[:, 0, par, 1, :].rearrange("p (k b f) -> p (k b) f", k=KD, b=FB)
                                  .rearrange("p (k b) f -> p k b f", k=KD),
                                  w1_raw[par].rearrange("p (k f b) -> p k b f", k=KD, b=FB),
                                  w_split[:, 0, par, 0, :].rearrange("p (k b f) -> p k b f", k=KD, b=FB).bitcast(F32),
                                  ALU.subtract).then_inc(w1_lo, 1)

            def low_w2(s, par):
                dve.wait_ge(w2_hi, s + 1)
                dve.tensor_tensor(w_split[:, 1, par, 1, :], w2_raw[par], w_split[:, 1, par, 0, :].bitcast(F32),
                                  ALU.subtract).then_inc(w2_lo, 1)

            def low_h(s, par, bank=6):
                dve.wait_ge(h_hi, s + 1)
                dve.tensor_tensor(slot_h[:, par, 1, :, :], banks[bank].rearrange("p (k n) -> p k n", k=KD),
                                  slot_h[:, par, 0, :, :].bitcast(F32), ALU.subtract).then_inc(h_lo, 1)

            def low_hid(s, par):
                for bank in range(BANKS):
                    dve.wait_ge(hid_hi, BANKS * s + bank + 1)
                    dve.tensor_tensor(hid[:, par, 1, 2 * bank:2 * bank + 2, :], relu[:, bank % 2, :, :],
                                      hid[:, par, 0, 2 * bank:2 * bank + 2, :].bitcast(F32),
                                      ALU.subtract).then_inc(hid_lo, 1)

            def finish(s, par, ring):
                e = dve.value_load(e_idx[0:1, bass.DynSlice(s, 1)], min_val=0, max_val=E - 1)
                if ring is not None:
                    dve.wait_ge(y_out[par], ring)
                dve.tensor_copy(dst_cur[:, par, :], dst_i[:, bass.DynSlice(TB * s, TB)]).then_inc(dst_ok, 1)
                dve.wait_ge(l2_done, s + 1)
                dve.tensor_tensor(y_sb[:, par, :, :], banks[4 + par].rearrange("p (t d) -> p t d", t=TB),
                                  b2_all[:, bass.DynSlice(e, 1), :].broadcast_to([P, TB, D]),
                                  ALU.add).then_inc(y_ok, 1)

            source(0, 0, None)
            source(1, 1, None)
            low_h(0, 0)
            low_h(1, 1, bank=7)
            dve.wait_ge(first_lo, 1)
            dve.sem_inc(w1_lo, 1)
            dve.wait_ge(exp_in, 32)
            def dve_step(s, par, gathered_by, scattered_by, first=False, turned=False):
                source(s + 2, par, gathered_by)
                if not first:
                    finish(s - 2, par, scattered_by)
                low_w1(s + 1, 1 - par)
                low_hid(s, par)
                if not turned:
                    low_h(s + 1, 1 - par)
                low_w2(s, par)

            for s in range(4):
                dve_step(s, s % 2, 32 * (s // 2) + 32, None, first=s < 2, turned=s == 0)
            with dve.Fori(2, LOOP.stop) as m:
                for par in range(2):
                    dve_step(2 * m + par, par, 32 * m + 32, 32 * m - 32)
            dve.wait_ge(grid_in, 64)
            A0, A1, B0, B1, B2 = (grid[:, n, :, :].rearrange("p q d -> p (q d)") for n in range(5))
            dve.tensor_scalar(dt_n[:, :], dt_b[:, :], -1.0, None, ALU.mult)
            dve.tensor_tensor(gr[:, 0, :], B1, A1, ALU.subtract)
            dve.tensor_tensor(gr[:, 1, :], B1, A1, ALU.add)
            ew = cst[:, C_EDGE:C_EDGE + 24].rearrange("p (n c) -> p n c", n=3)
            for at, cols in ((slice(0, 4), slice(0, 4)), (slice(4, 8), slice(D - 4, D))):
                for n, gi, dst in ((0, 3, edge_w[:, 0, 0:KD, at]), (1, 1, edge_t[:, :, at]),
                                   (2, 4, edge_w[:, 1, 0:KD, at])):
                    last = dve.tensor_tensor(dst, grid[:, gi, :, cols], ew[:, n:n + 1, at].broadcast_to([P, KD, 4]),
                                             ALU.mult)
            link(last)
            link(dve.tensor_tensor(edge_w[:, 0, 0:KD, :], edge_w[:, 0, 0:KD, :], edge_t[:, :, :], ALU.add))
            dve.tensor_copy(edge_w[:, :, KD:2 * KD, :], edge_w[:, :, 0:KD, :])
            dve.tensor_scalar(gr[:, 2, :], B2, 0.5, None, ALU.mult)
            dve.tensor_scalar(gr[:, 0:2, :], gr[:, 0:2, :], 0.5, None, ALU.mult).then_inc(grids_ok, 1)

            last_round = (NS - 1) // 2
            finish(NS - 3, 0, 32 * (last_round - 1))
            low_hid(NS - 1, 0)
            low_w2(NS - 1, 0)
            finish(NS - 2, 1, 32 * (last_round - 1))
            finish(NS - 1, 0, 32 * last_round)

            dve.wait_ge(grids_ok, 1)

            def edge_cols(v):
                return v[:, :, 0:4], v[:, :, D - 4:D]

            def add_up(g):
                dve.wait_ge(y_in[g % 2], 32 * (g // 2 + 1))
                y1, y2, f, f0 = (v[g % 2].rearrange("p (j d) -> p j d", j=4) for v in (Y1, Y2, FV, F0))
                if g >= 2:
                    dve.wait_ge(t_fd, g - 1)
                for j in range(4):
                    last = dve.scalar_tensor_tensor(out=f0[:, j, :], in0=y1[:, j, :],
                                                    scalar=gates[:, 0, 4 * g + j:4 * g + j + 1],
                                                    in1=x_sb[:, 4 * g + j, :], op0=ALU.mult, op1=ALU.add)
                link(last)
                for j in range(4):
                    last = dve.scalar_tensor_tensor(out=f[:, j, :], in0=y2[:, j, :],
                                                    scalar=gates[:, 1, 4 * g + j:4 * g + j + 1],
                                                    in1=f0[:, j, :], op0=ALU.mult, op1=ALU.add)
                last.then_inc(t_f, 1)
                dve.wait_ge(t_f, g + 1)

            def wide(v):
                return v.rearrange("p (i n) -> p i n", i=2)

            def over(v):
                return v.rearrange("p (a n) -> p a n", a=1).broadcast_to([P, 2, 512])

            def rows_of(v):
                return v.rearrange("p (r d) -> p r d", d=D)

            def products(g):
                par = g % 2
                f, a, b, u1 = FD[par], PA[par], PB[par], U1[par]
                if g >= 2:
                    dve.wait_ge(t_mm, g - 1)
                dve.wait_ge(t_keep, g + 1)
                dve.tensor_tensor(GF[par], GG[par], FV[par], ALU.mult)
                dve.wait_ge(t_fd, g + 1)
                dve.tensor_tensor(wide(a), over(A0), wide(f), ALU.mult)
                dve.tensor_tensor(wide(b), over(gr[:, 2, :]), wide(f), ALU.mult)
                for kind in range(2):
                    for side, fe in enumerate(edge_cols(rows_of(f))):
                        last = dve.tensor_tensor(edge_p[:, par, kind, :, side, :], fe,
                                                 edge_w[:, kind, :, 4 * side:4 * side + 4], ALU.mult)
                link(last)
                bv, cv = rows_of(b), rows_of(CC[par])
                dve.tensor_reduce(cv[:, :, 0:D:D - 1], edge_p[:, par, 1, :, :, :], AX_X, ALU.add)
                dve.tensor_reduce(rows_of(SM[par])[:, :, 0:D:D - 1], edge_p[:, par, 0, :, :, :], AX_X, ALU.add)
                link(dve.tensor_tensor(cv[:, :, 1:D - 1], bv[:, :, 2:D], bv[:, :, 0:D - 2], ALU.subtract))
                dve.tensor_tensor(u1, CC[par], a, ALU.subtract).then_inc(t_u1, 1)

            def update(g):
                par = g % 2
                pv, qv = rows_of(PP[par]), rows_of(PQ[par])
                if g == NPAIR - 1:
                    dve.tensor_tensor(wide(PP[par]), over(gr[:, 0, :]), wide(FD[par]), ALU.mult)
                    link(dve.tensor_tensor(wide(PQ[par]), over(gr[:, 1, :]), wide(FD[par]), ALU.mult))
                else:
                    dve.wait_ge(t_p, g + 1)
                    dve.wait_ge(t_q, g + 1)
                link(dve.tensor_tensor(rows_of(SM[par])[:, :, 1:D - 1], pv[:, :, 2:D], qv[:, :, 0:D - 2], ALU.add))
                dve.wait_ge(t_mm, g + 1)
                if g >= 2:
                    dve.wait_ge(t_relu, g - 1)
                at = 2 * par
                last = dve.tensor_tensor(TT[par].rearrange("p (i q d) -> p q i d", i=2, q=2),
                                         psum[:, at:at + 2, :].rearrange("p q (i d) -> p q i d", i=2),
                                         SM[par].rearrange("p (i q d) -> p q i d", i=2, q=2), ALU.add)
                last.then_inc(t_fin, 1)

            for g in range(NPAIR + 1):
                if g < NPAIR:
                    add_up(g)
                    products(g)
                if g >= 1:
                    update(g - 1)


_INS = ['x', 'itok_B_6_14', 'condB_dt', 'L0_cond_exp_w1', 'L0_cond_exp_b1', 'L0_cond_exp_w2', 'L0_cond_exp_b2',
        'L1_cond_A_grid', 'L1_cond_B_grid']


def kernel(**inputs):
    import concourse.bacc as _bacc
    from concourse.bass_utils import run_bass_kernel_spmd as _run

    nc = _bacc.Bacc("TRN2", target_bir_lowering=False, num_devices=1)
    arrays, args = {}, []
    given = {name: np.ascontiguousarray(inputs[name]) for name in _INS}
    for name, a in {**given, "small": pack(inputs), "constants": constants()}.items():
        arrays[f"in_{name}_dram"] = a
        args.append(nc.dram_tensor(f"in_{name}_dram", a.shape, mybir.dt.from_np(a.dtype), kind="ExternalInput").ap())
    args.append(nc.dram_tensor("out_0_dram", (NB, T, D), F32, kind="ExternalOutput").ap())
    moe_then_stencil(nc, *args)
    r = _run(nc, [arrays], core_ids=[0])
    return r.results[0]["out_0_dram"]
```

```python
from contextlib import ExitStack

import numpy as np

import concourse.bass as bass
from concourse import mybir

ALU = mybir.AluOpType
ACT = mybir.ActivationFunctionType
F32 = mybir.dt.float32
F32R = mybir.dt.float32r
BF16 = mybir.dt.bfloat16
I32 = mybir.dt.int32
AX_X = mybir.AxisListType.X

P = 128
NB, T, D = 8, 256, 256
N = NB * T
NJ = N // P
KD = D // P
E, FF, TOPK = 8, 1024, 2
S_SUB, SE, SH = 32, 64, 128
FB = FF // P
ST = 256
TB = ST // P
NS = N * TOPK // ST + E - 1
NC = NS * TB
BANKS = FB // 2
EMPTY = 8192.0

C_IDENT = 0
C_PART = C_IDENT + P
C_BEFORE = C_PART + 2
C_EXPERT = C_BEFORE + P
C_SLOT = C_EXPERT + NJ * E
C_FRONT = C_SLOT + NS * E
C_D1 = C_FRONT
C_D2 = C_D1 + KD * T
C_EDGE = C_D2 + KD * T
C_ALL = C_EDGE + 24


def stencil(n):
    d1, d2 = np.zeros((n, n)), np.zeros((n, n))
    for i in range(1, n - 1):
        d1[i, i - 1], d1[i, i + 1] = -0.5, 0.5
        d2[i, i - 1], d2[i, i], d2[i, i + 1] = 1, -2, 1
    d1[0, :3] = [-1.5, 2, -0.5]
    d1[-1, -3:] = [0.5, -2, 1.5]
    d2[0, :4] = [2, -5, 4, -1]
    d2[-1, -4:] = [-1, 4, -5, 2]
    return d1, d2


def constants():
    c = np.zeros((P, C_ALL), np.float32)
    p = np.arange(P)
    c[:, C_IDENT:C_IDENT + P] = np.eye(P)
    c[:, C_BEFORE:C_BEFORE + P] = p[:, None] < p[None, :]
    c[:, C_EXPERT:C_EXPERT + NJ * E] = np.tile(np.arange(E), NJ)
    c[:, C_SLOT:C_SLOT + NS * E] = np.repeat(np.arange(NS), E)
    c[:, C_PART] = p
    c[:, C_PART + 1] = p + 1
    d1, d2 = stencil(T)
    c[:, C_D1:C_D1 + KD * T] = d1.T.reshape(KD, P, T).transpose(1, 0, 2).reshape(P, -1)
    c[:, C_D2:C_D2 + KD * T] = 0.5 * d2.T.reshape(KD, P, T).transpose(1, 0, 2).reshape(P, -1)
    for n, (m, w, own) in enumerate(((d2, 0.5, 1.0), (d1, -1.0, 0.0), (d1, 1.0, 0.0))):
        c[:, C_EDGE + 8 * n:C_EDGE + 8 * n + 4] = w * m[0, :4]
        c[:, C_EDGE + 8 * n + 4:C_EDGE + 8 * n + 8] = w * m[-1, -4:]
        c[:, C_EDGE + 8 * n] += own
        c[:, C_EDGE + 8 * n + 7] += own
    return c


SMALL = {}
for _name, _rows, _cols in (("ln_g", P, KD), ("ln_b", P, KD), ("router_w", P, KD * E), ("hyp_b1", SH, 1),
                            ("hyp_b2", SH, 1), ("sty_b1", SH // 2, 1), ("sty_b2", P, 2 * D // P),
                            ("subj_emb", S_SUB, SE), ("hyp_w1", SE, SH), ("hyp_w2", SH, SH),
                            ("sty_w1", SH, SH // 2), ("sty_w2", SH // 2, 2 * D)):
    SMALL[_name] = (_rows, _cols, sum(v[1] for v in SMALL.values()))
SMALL_ALL = sum(v[1] for v in SMALL.values())


def pack(inputs):
    out = np.zeros((P, SMALL_ALL), np.float32)
    for name, (rows, cols, at) in SMALL.items():
        a = np.asarray(inputs["L0_cond_" + name])
        if name == "router_w":
            a = a.reshape(KD, P, E).transpose(1, 0, 2)
        elif a.ndim == 1 and cols > 1:
            a = a.reshape(cols, P).T
        out[:rows, at:at + cols] = a.reshape(rows, cols)
    return out


def moe_then_stencil(nc, x, ids, dt, exp_w1, exp_b1, exp_w2, exp_b2, a_grid, b_grid, small, consts, out):
    h_rows = nc.dram_tensor("h_rows", (N, D), F32, kind="Internal").ap()
    y_rows = nc.dram_tensor("y_rows", (TOPK * N, D), F32, kind="Internal").ap()

    ctx = ExitStack()
    with ctx:
        def sb(name, shape, dt_=F32):
            return ctx.enter_context(nc.sbuf_tensor(name, shape, dt_))

        def sem(name):
            return ctx.enter_context(nc.semaphore(name))

        psum = ctx.enter_context(nc.psum_tensor("psum", [P, 8, 512], F32))
        banks = [psum[:, i, :] for i in range(8)]

        x_sb = sb("x_sb", [P, NJ, D])
        cst = sb("cst", [P, C_ALL])
        ident = cst[:, C_IDENT:C_IDENT + P]
        gates = sb("gates", [P, TOPK, NJ])
        mx = sb("mx", [P, TOPK, NJ])
        dst_i = sb("dst_i", [P, NC], I32)
        src_i = sb("src_i", [P, NC + TB], I32)
        e_idx = sb("e_idx", [1, NS], I32)
        ones8 = sb("ones8", [P, E])
        b2_all = sb("b2_all", [P, E, D])
        b1_all = sb("b1_all", [P, E, FB])
        grid = sb("grid", [P, 5, KD, D])
        gr = sb("gr", [P, 3, KD * D])
        dt_b = sb("dt_b", [P, NB])
        dt_n = sb("dt_n", [P, NB])
        edge_w = sb("edge_w", [P, 2, 2 * KD, 8])
        edge_t = sb("edge_t", [P, KD, 8])

        with ExitStack() as phase:
            def own(name, shape, dt_=F32):
                return phase.enter_context(nc.sbuf_tensor(name, shape, dt_))

            raw_a = own("raw_a", [P, 2, 2048])
            raw_b = own("raw_b", [P, 2, 2048])
            w_split = own("w_split", [P, 2, 2, 2, 2048], F32R)
            hid = own("hid", [P, 2, 2, FB, ST], F32R)
            relu = own("relu", [P, 2, 2, ST])
            slot_h = own("slot_h", [P, 2, 2, KD, ST], F32R)
            gathered = own("gathered", [P, 2, TB, D])
            y_sb = own("y_sb", [P, 2, TB, D])
            b1_cur = own("b1_cur", [P, 2, FB])
            src_cur = own("src_cur", [P, 2, TB], I32)
            dst_cur = own("dst_cur", [P, 2, TB], I32)
        w1_raw = [raw_a[:, i, :] for i in range(2)]
        w2_raw = [raw_b[:, i, :] for i in range(2)]

        with ExitStack() as phase:
            def own(name, shape, dt_=F32):
                return phase.enter_context(nc.sbuf_tensor(name, shape, dt_))

            h_pre = own("h_pre", [P, KD, N])
            hT = own("hT", [P, KD, N])
            own("w_split_first", [P, 10240])
            z = own("z", [P, 4, D])
            tok = own("tok", [P, 2, NC, TOPK * NJ], BF16)
            own("w_split_last", [P, 6144 - 1024 - TOPK * NJ * NC])
            h_tok = own("h_tok", [P, NJ, KD, P + E])
            oh_row = own("oh_row", [P, P, TOPK * NJ], BF16)
            oh_col = own("oh_col", [P, NC, TOPK * NJ], BF16)
            eye_rw = own("eye_rw", [P, KD, P + E])
            before_bf = own("before_bf", [P, P], BF16)
            ones_bf = own("ones_bf", [P, P], BF16)
            st1 = own("st1", [P, NJ, 6])
            mv1 = own("mv1", [P, NJ, 2])
            var1 = own("var1", [P, NJ])
            rs1 = own("rs1", [P, NJ])
            st2 = own("st2", [P, NB, KD, 6])
            mv2 = own("mv2", [P, NB, KD, 2])
            var2 = own("var2", [P, NB, KD])
            rs2 = own("rs2", [P, NB, KD])
            half = own("half", [P, 8])
            warm = own("warm", [P, 8])
            aff_a = own("aff_a", [P, NB, KD])
            aff_m = own("aff_m", [P, NB, KD])
            aff_b = own("aff_b", [P, NB, KD])
            id_i = own("id_i", [S_SUB, NB], I32)
            id_f = own("id_f", [S_SUB, NB])
            oh_s = own("oh_s", [S_SUB, NB])
            small_sb = own("small_sb", [P, SMALL_ALL])
            se_t = own("se_t", [SE, NB])
            hy1 = own("hy1", [SH, NB])
            hy2 = own("hy2", [SH, NB])
            sy1 = own("sy1", [SH // 2, NB])
            sty = own("sty", [P, 4, NB])
            gabs = own("gabs", [P, KD, NB])
            grelu = own("grelu", [P, KD, NB])
            gexp = own("gexp", [P, KD, NB])
            gln = own("gln", [P, KD, NB])
            gsum = own("gsum", [P, KD, NB])
            gam = own("gam", [P, KD, NB])
            lg = own("lg", [P, NJ, E])
            eq = own("eq", [P, NJ, E])
            cand = own("cand", [P, NJ, E])
            least = own("least", [P, NJ])
            oh = own("oh", [P, TOPK, NJ, E])
            lg2 = own("lg2", [P, NJ, E])
            gap = own("gap", [P, NJ])
            e2 = own("e2", [P, NJ])
            den = own("den", [P, NJ])
            m_bf = own("m_bf", [P, NJ, E], BF16)
            cnt_i = own("cnt_i", [P, E], I32)
            tl_i = own("tl_i", [P, E], I32)
            tl_f = own("tl_f", [P, E])
            t_end = own("t_end", [P, E])
            t_off = own("t_off", [P, E])
            base = own("base", [P, E])
            pos = own("pos", [P, NJ, E])
            pick = own("pick", [P, TOPK, NJ, E])
            slot_f = own("slot_f", [P, TOPK * NJ])
            slot_i = own("slot_i", [P, TOPK * NJ], I32)
            low_i = own("low_i", [P, TOPK * NJ], I32)
            col_i = own("col_i", [P, TOPK * NJ], I32)
            low_f = own("low_f", [P, TOPK * NJ], BF16)
            col_f = own("col_f", [P, TOPK * NJ], BF16)
            row_of = own("row_of", [P, P, TOPK * NJ], BF16)
            col_of = own("col_of", [P, NC, TOPK * NJ], BF16)
            tile_of = own("tile_of", [P, TOPK * NJ], BF16)
            e_cmp = own("e_cmp", [1, NS, E])
            e_sum = own("e_sum", [1, NS])
            num_i = own("num_i", [P, NC], I32)
            num_f = own("num_f", [P, NC])

        def part(name):
            rows, cols, at = SMALL[name]
            return small_sb[0:rows, at:at + cols]

        rw_sb = part("router_w").rearrange("p (k e) -> p k e", k=KD)
        emb, hw1, hw2, sw1, sw2 = (part(n) for n in ("subj_emb", "hyp_w1", "hyp_w2", "sty_w1", "sty_w2"))
        hb1, hb2, sbi1, sbi2 = (part(n) for n in ("hyp_b1", "hyp_b2", "sty_b1", "sty_b2"))
        ln_gain, ln_offset = part("ln_g"), part("ln_b")

        with ExitStack() as phase:
            def own(name, shape, dt_=F32):
                return phase.enter_context(nc.sbuf_tensor(name, shape, dt_))

            Y1, Y2, F0, FV, FD, GG, GF, PA, PB, CC, U1, U2, PP, PQ, SM, OUT = (
                [own(f"{n}_{par}", [P, 4 * D])[:, :] for par in range(2)]
                for n in ("t_y1", "t_y2", "t_f0", "t_f", "t_fd", "t_keep", "t_kept", "t_a0f", "t_b2f", "t_d1b2f",
                          "t_u1", "t_b0f", "t_pf", "t_qf", "t_cols", "t_out"))
            edge_p = own("edge_p", [P, 2, 2, 4, 2, 4])

        x_in = [sem(f"x_in{i}") for i in range(4)]
        ident_in, cst_in = sem("ident_in"), sem("cst_in")
        sty_in = sem("sty_in")
        exp_in = sem("exp_in")
        grid_in = sem("grid_in")
        chain = sem("chain")
        half_set = sem("half_set")
        var1_ok = sem("var1_ok")
        rs1_ok = sem("rs1_ok")
        z_ok = sem("z_ok")
        fwd_t = sem("fwd_t")
        pre_ok = sem("pre_ok")
        var2_ok = sem("var2_ok")
        rs2_ok = sem("rs2_ok")
        aff_ok, ht_ok = sem("aff_ok"), sem("ht_ok")
        eye_ok, iota_ok = sem("eye_ok"), sem("iota_ok")
        back_t = sem("back_t")
        htok_ok, htok_late = sem("htok_ok"), sem("htok_late")
        hrows_out = sem("hrows_out")
        sty_pe = sem("sty_pe")
        sty_act = sem("sty_act")
        sty_dve = sem("sty_dve")
        gap_ok = sem("gap_ok")
        e2_ok = sem("e2_ok")
        m_ok = sem("m_ok")
        rank_ok = sem("rank_ok")
        ohcol_ok = sem("ohcol_ok")
        tok0_ok, tok_ok = sem("tok0_ok"), sem("tok_ok")
        ohrow_ok = sem("ohrow_ok")
        perm_mm = sem("perm_mm")
        e_ok = sem("e_ok")
        w1_in = [sem(f"w1_in{i}") for i in range(2)]
        w2_in = [sem(f"w2_in{i}") for i in range(2)]
        w1_hi, w1_lo, w2_hi, w2_lo = sem("w1_hi"), sem("w1_lo"), sem("w2_hi"), sem("w2_lo")
        h_hi, h_lo = sem("h_hi"), sem("h_lo")
        b1_ok = sem("b1_ok")
        l1_done, relu_ok, hid_hi, hid_lo, l2_done = (sem("l1_done"), sem("relu_ok"), sem("hid_hi"),
                                                     sem("hid_lo"), sem("l2_done"))
        pool_go = sem("pool_go")
        tr_done, y_ok = sem("tr_done"), sem("y_ok")
        l2_half, y_half = sem("l2_half"), sem("y_half")
        src_ok, dst_ok = sem("src_ok"), sem("dst_ok")
        rows_in = [sem(f"rows_in{i}") for i in range(2)]
        y_out = [sem(f"y_out{i}") for i in range(2)]

        y_in = [[sem(f"y{c}_in{i}") for i in range(2)] for c in range(TOPK)]
        y_first = [[sem(f"y{c}_first{i}") for i in range(2)] for c in range(TOPK)]
        t_first = sem("t_first")
        t_f, t_u2, t_p, t_q = (sem(n) for n in ("t_f", "t_u2", "t_p", "t_q"))
        t_u1, t_s, t_gf0, t_gf, t_mm, t_relu = (sem(n) for n in ("t_u1", "t_s", "t_gf0", "t_gf", "t_mm", "t_relu"))
        t_keep, t_fd, t_gated = sem("t_keep"), sem("t_fd"), sem("t_gated")
        out_dma = [sem(f"out_dma{i}") for i in range(3)]
        grids_ok = sem("grids_ok")

        x_tok = x.rearrange("b (q p) d -> p (b q) d", p=P)
        out_tok = out.rearrange("b (q p) d -> p (b q) d", p=P)
        h_rows_tok = h_rows.rearrange("(j p) d -> p j d", p=P)
        y_rows_tok = y_rows.rearrange("(c j p) d -> c p j d", c=TOPK, p=P)
        w1_of = exp_w1.rearrange("e (k p) f -> p e k f", p=P)
        w2_of = exp_w2.rearrange("e (p b) d -> p e (b d)", b=FB)

        block = ctx.enter_context(nc.Block())

        NPAIR = NB // 2
        LOOP = range(1, (NS - 1) // 2)
        assert NS % 2 == 1
        STYLE = 5
        CHUNK = 8
        LATE = NB // 2

        def rows_taken(b):
            return (htok_ok, b + 1) if b < LATE else (htok_late, b + 1 - LATE)

        JOINED = (2, 3)

        def kept(g):
            return (t_gf0, 1) if g == 0 else (t_gf, g)

        @block.sync
        def _(sp):
            for i in range(4):
                sp.dma_start(x_sb[:, 4 * i:4 * i + 4, :], x_tok[:, 4 * i:4 * i + 4, :]).then_inc(x_in[i], 16)
                if i == 0:
                    sp.dma_start(small_sb[:, :], small).then_inc(sty_in, 16)
            for b in range(NB):
                sp.wait_ge(*rows_taken(b))
                for j in range(2 * b, 2 * b + 2):
                    sp.dma_start(h_rows_tok[:, j, :].rearrange("p (k n) -> p k n", k=KD),
                                 h_tok[:, j, :, 0:P]).then_inc(hrows_out, 16)

            def weights(s, par):
                e = sp.value_load(e_idx[0:1, bass.DynSlice(s, 1)], min_val=0, max_val=E - 1)
                sp.wait_ge(w1_hi, s - 1)
                sp.wait_ge(w1_lo, s - 1)
                sp.dma_start(w1_raw[par].rearrange("p (k f) -> p k f", k=KD),
                             w1_of[:, bass.DynSlice(e, 1), :, :].rearrange("p e k f -> p (e k) f")
                             ).then_inc(w1_in[par], 16)
                sp.wait_ge(w2_hi, s - 1)
                sp.wait_ge(w2_lo, s - 1)
                sp.dma_start(w2_raw[par], w2_of[:, bass.DynSlice(e, 1), :].rearrange("p e n -> p (e n)")
                             ).then_inc(w2_in[par], 16)

            sp.wait_ge(e_ok, 1)
            sp.wait_ge(back_t, NB)
            first_e = [sp.value_load(e_idx[0:1, s:s + 1], min_val=0, max_val=E - 1) for s in range(2)]
            for s in range(2):
                sp.dma_start(w1_raw[s].rearrange("p (k f) -> p k f", k=KD),
                             w1_of[:, bass.DynSlice(first_e[s], 1), :, :].rearrange("p e k f -> p (e k) f")
                             ).then_inc(w1_in[s], 16)
            sp.wait_ge(rows_in[0], 32)
            for s in range(2):
                sp.dma_start(w2_raw[s], w2_of[:, bass.DynSlice(first_e[s], 1), :].rearrange("p e n -> p (e n)")
                             ).then_inc(w2_in[s], 16)
            with sp.Fori(1, LOOP.stop) as m:
                for par in range(2):
                    weights(2 * m + par, par)
            weights(NS - 1, 0)

            sp.wait_ge(l2_done, NS)
            for par in range(2):
                sp.wait_ge(y_out[par], 32 * ((NS + 1 - par) // 2))
            for i in range(2):
                for c, buf in enumerate((Y1, Y2)):
                    sp.dma_start(buf[0][:, 2 * D * i:2 * D * i + 2 * D].rearrange("p (j d) -> p j d", j=2),
                                 y_rows_tok[c, :, 2 * i:2 * i + 2, :]).then_inc(y_first[c][i], 16)
            for g in range(1, NPAIR):
                if g >= 2:
                    sp.wait_ge(t_f, g - 1)
                for c, buf in enumerate((Y1, Y2)):
                    sp.dma_start(buf[g % 2].rearrange("p (j d) -> p j d", j=4),
                                 y_rows_tok[c, :, 4 * g:4 * g + 4, :]).then_inc(y_in[c][g % 2], 16)
            for g in range(NPAIR - 1):
                sp.wait_ge(t_relu, g + 1)
                sp.dma_start(out_tok[:, 4 * g:4 * g + 4, :],
                             OUT[g % 2].rearrange("p (j d) -> p j d", j=4)).then_inc(out_dma[g % 2], 16)
            g = NPAIR - 1
            for q in range(2):
                sp.wait_ge(t_relu, NPAIR + q)
                sp.dma_start(out_tok[:, 4 * g + q:4 * g + 4:2, :],
                             OUT[g % 2].rearrange("p (i q d) -> p q i d", i=2, q=2)[:, q]).then_inc(out_dma[2], 16)
            sp.wait_ge(out_dma[0], 16 * (NPAIR // 2))
            sp.wait_ge(out_dma[1], 16 * (NPAIR // 2 - 1))
            sp.wait_ge(out_dma[2], 32)
            sp.wait_ge(hrows_out, 16 * NJ)

        @block.scalar
        def _(act):
            def load(dst, src, s):
                act.dma_start(dst, src).then_inc(s, 16)

            load(id_i[:, :], ids.rearrange("(a b) -> a b", a=1).partition_broadcast(S_SUB), sty_in)
            load(cst[:, 0:C_BEFORE], consts[:, 0:C_BEFORE], ident_in)
            load(cst[:, C_BEFORE:C_FRONT], consts[:, C_BEFORE:C_FRONT], cst_in)

            act.wait_ge(half_set, 1)
            act.activation(warm[:, :], half[:, :], ACT.Copy)

            def style(i):
                act.wait_ge(sty_pe, i + 1)
                if i == 0:
                    last = act.activation(se_t[:, :], banks[1][0:SE, 0:NB], ACT.Copy)
                elif i == 1:
                    last = act.activation(hy1[:, :], banks[1][:, 8:8 + NB], ACT.Relu, bias=hb1[:, 0:1])
                elif i == 2:
                    last = act.activation(hy2[:, :], banks[1][:, 16:16 + NB], ACT.Identity, bias=hb2[:, 0:1])
                elif i == 3:
                    last = act.activation(sy1[:, :], banks[1][0:SH // 2, 24:24 + NB], ACT.Relu, bias=sbi1[:, 0:1])
                else:
                    for c in range(4):
                        last = act.activation(sty[:, c, :], banks[1][:, 32 + 8 * c:40 + 8 * c], ACT.Identity,
                                              bias=sbi2[:, c:c + 1])
                last.then_inc(sty_act, 1)

            def front(b):
                act.wait_ge(fwd_t, b + 1)
                for k in range(KD):
                    last = act.activation(h_pre[:, k, T * b:T * b + T], banks[4 + b % 2][:, T * k:T * k + T],
                                          ACT.Identity, bias=ln_offset[:, k:k + 1], scale=ln_gain[:, k:k + 1])
                last.then_inc(pre_ok, 1)

            def styled(b):
                act.wait_ge(aff_ok, b + 1)
                for k in range(KD):
                    last = act.activation(hT[:, k, T * b:T * b + T], h_pre[:, k, T * b:T * b + T], ACT.Identity,
                                          bias=aff_b[:, b, k:k + 1], scale=aff_a[:, b, k:k + 1])
                last.then_inc(ht_ok, 1)

            def rows(b):
                act.wait_ge(back_t, b + 1)
                at = 6 if b % 2 == 0 else 2
                act.activation(h_tok[:, 2 * b:2 * b + 2, :, :],
                               psum[:, at:at + 2, 0:KD * (P + E)].rearrange("p j (k n) -> p j k n", k=KD),
                               ACT.Copy).then_inc(htok_ok, 1)

            for i in range(NB + 4):
                if 3 <= i < NB + 3:
                    styled(i - 3)
                if i == 0:
                    act.wait_ge(sty_in, 32)
                if i < NB:
                    front(i)
                if i == 0:
                    for n in range(STYLE):
                        style(n)
                    act.wait_ge(sty_act, 5)
                    act.activation(gabs[:, :, :], sty[:, 0:KD, :], ACT.Abs).then_inc(sty_act, 1)
                    act.wait_ge(sty_act, 6)
                    act.activation(gexp[:, :, :], gabs[:, :, :], ACT.Exp, scale=-1.0).then_inc(sty_act, 1)
                    act.wait_ge(sty_act, 7)
                    act.activation(gln[:, :, :], gexp[:, :, :], ACT.Ln, bias=ones8[:, 0:1]).then_inc(sty_act, 1)
                if 0 <= i - 4 < LATE:
                    rows(i - 4)
                if i == 4:
                    load(cst[:, C_FRONT:C_ALL], consts[:, C_FRONT:C_ALL], grid_in)
                    load(b1_all[:, :, :], exp_b1.rearrange("e (p b) -> p e b", b=FB), exp_in)
                    load(b2_all[:, :, :], exp_b2.rearrange("(a e) d -> a e d", a=1).partition_broadcast(P), exp_in)
                    load(grid[:, 0:2, :, :], a_grid.rearrange("g (q p) d -> p g q d", p=P), grid_in)
                    load(grid[:, 2:5, :, :], b_grid.rearrange("g (q p) d -> p g q d", p=P), grid_in)
                    load(dt_b[:, :], dt.rearrange("(a b) -> a b", a=1).partition_broadcast(P), grid_in)

            act.wait_ge(gap_ok, 1)
            act.activation(e2[:, :], gap[:, :], ACT.Exp).then_inc(e2_ok, 1)
            act.wait_ge(ohcol_ok, 1)
            act.activation(tok[:, 0, :, :], oh_col[:, :, :], ACT.Copy,
                           scale=cst[:, C_PART + 1:C_PART + 2]).then_inc(tok0_ok, 1)

            def split_w1(s, par, landed, first=False):
                act.wait_ge(w1_in[par], landed)
                if not first:
                    act.wait_ge(l1_done, BANKS * (s - 1))
                act.activation(w_split[:, 0, par, 0, :].rearrange("p (k b f) -> p k b f", k=KD, b=FB),
                               w1_raw[par].rearrange("p (k f b) -> p k b f", k=KD, b=FB),
                               ACT.Copy).then_inc(w1_hi, 1)

            def split_w2(s, par, landed, first=False):
                act.wait_ge(w2_in[par], landed)
                if not first:
                    act.wait_ge(l2_done, s - 1)
                act.activation(w_split[:, 1, par, 0, :], w2_raw[par], ACT.Copy).then_inc(w2_hi, 1)

            def split_h(s, par, first=False, bank=6):
                act.wait_ge(tr_done, s + 1)
                if not first:
                    act.wait_ge(l1_done, BANKS * (s - 1))
                act.activation(slot_h[:, par, 0, :, :], banks[bank].rearrange("p (k n) -> p k n", k=KD),
                               ACT.Copy).then_inc(h_hi, 1)

            def step(s, par, landed, begin=BANKS, last_slot=False):
                e = act.value_load(e_idx[0:1, bass.DynSlice(s, 1)], min_val=0, max_val=E - 1)
                act.activation(b1_cur[:, par, :],
                               b1_all[:, bass.DynSlice(e, 1), :].rearrange("p e b -> p (e b)"),
                               ACT.Copy).then_inc(b1_ok, 1)
                act.wait_ge(b1_ok, s + 1)
                if not last_slot and begin > 0:
                    split_w1(s + 1, 1 - par, landed + 16 * par)
                if begin == 0:
                    split_w2(s, par, landed, first=True)
                for bank in range(BANKS):
                    act.wait_ge(l1_done, BANKS * s + bank + 1)
                    if begin > 0 or bank >= 2:
                        act.wait_ge(hid_lo, BANKS * s + bank - 1)
                    for i in range(2):
                        blk = 2 * bank + i
                        last = act.activation(relu[:, bank % 2, i, :], banks[bank][:, ST * i:ST * i + ST],
                                              ACT.Relu, bias=b1_cur[:, par, blk:blk + 1])
                    last.then_inc(relu_ok, 1)
                if not last_slot and begin > 0:
                    split_h(s + 1, 1 - par)
                if begin > 0:
                    split_w2(s, par, landed, first=begin < 2)

            act.wait_ge(exp_in, 32)
            act.wait_ge(e_ok, 1)
            split_w1(0, 0, 16, first=True)
            split_w1(1, 1, 16, first=True)
            split_h(0, 0, first=True)
            split_h(1, 1, first=True, bank=7)
            step(0, 0, 16, begin=0)
            step(1, 1, 16, begin=1)
            with act.Fori(1, LOOP.stop) as m:
                for par in range(2):
                    step(2 * m + par, par, 16 * m + 16)
            step(NS - 1, 0, 16 * ((NS - 1) // 2) + 16, last_slot=True)

            def relu_out(g):
                act.wait_ge(t_mm, g + 1)
                if g >= 2:
                    act.wait_ge(out_dma[g % 2], 16 * (g // 2))
                act.activation(OUT[g % 2].rearrange("p (i q d) -> p q i d", i=2, q=2),
                               psum[:, 2 * g:2 * g + 2, :].rearrange("p q (i d) -> p q i d", i=2),
                               ACT.Relu).then_inc(t_relu, 1)

            act.wait_ge(grids_ok, 1)
            act.wait_ge(l2_done, NS)
            act.wait_ge(y_ok, NS)

            def keep(g):
                if g >= 2:
                    act.wait_ge(*kept(g - 2))
                for i in range(2):
                    last = act.activation(GG[g % 2][:, 512 * i:512 * i + 512],
                                          grid[:, 3, :, :].rearrange("p q d -> p (q d)"), ACT.Identity,
                                          bias=ones8[:, 0:1], scale=dt_n[:, 2 * g + i:2 * g + i + 1])
                last.then_inc(t_keep, 1)

            def gated(g):
                for c, y in enumerate((Y1, Y2)):
                    act.wait_ge(y_in[c][g % 2], 16 * ((g + 1) // 2))
                    for j in range(4):
                        yj = y[g % 2][:, D * j:D * j + D]
                        last = act.activation(yj, yj, ACT.Copy, scale=gates[:, c, 4 * g + j:4 * g + j + 1])
                    last.then_inc(t_gated, 1)

            keep(0)
            for g in range(NPAIR):
                if g >= 2:
                    act.wait_ge(t_s, g - 1)
                    act.wait_ge(t_u2, g - 1)
                for i in range(2):
                    if g == 0 and i == 0:
                        act.wait_ge(t_first, 1)
                    else:
                        act.wait_ge(t_f, g + 1)
                    last = act.activation(FD[g % 2][:, 512 * i:512 * i + 512], FV[g % 2][:, 512 * i:512 * i + 512],
                                          ACT.Copy, scale=dt_b[:, 2 * g + i:2 * g + i + 1])
                last.then_inc(t_fd, 1)
                if g < NPAIR - 1:
                    keep(g + 1)
                    gated(g + 1)
                if g >= 1:
                    relu_out(g - 1)
            for q in range(2):
                act.wait_ge(t_mm, NPAIR + q)
                if q == 0:
                    act.wait_ge(out_dma[(NPAIR - 1) % 2], 16 * ((NPAIR - 1) // 2))
                act.activation(OUT[(NPAIR - 1) % 2].rearrange("p (i q d) -> p q i d", i=2, q=2)[:, q],
                               banks[2 * NPAIR - 2 + q].rearrange("p (i d) -> p i d", i=2),
                               ACT.Relu).then_inc(t_relu, 1)

        @block.gpsimd
        def _(pool):
            pool.memset(half[:, :], -0.5).then_inc(half_set, 1)
            pool.wait_ge(half_set, 1)

            def number(out, pattern):
                pool.iota(out, pattern=pattern, base=0, channel_multiplier=0,
                          allow_small_or_imprecise_dtypes=True).then_inc(iota_ok, 1)

            for i in range(NB + 3):
                if i < NB:
                    pool.wait_ge(var1_ok, i + 1)
                    pool.tensor_tensor(rs1[:, 2 * i:2 * i + 2], var1[:, 2 * i:2 * i + 2], half[:, 0:2],
                                       ALU.pow).then_inc(rs1_ok, 1)
                if i >= 3:
                    pool.wait_ge(var2_ok, i - 2)
                    pool.tensor_tensor(rs2[:, i - 3, :], var2[:, i - 3, :], half[:, 0:KD],
                                       ALU.pow).then_inc(rs2_ok, 1)
            number(tile_of[:, :], [[P, TOPK * NJ]])
            number(col_of[:, :, :], [[1, NC], [0, TOPK * NJ]])
            number(row_of[:, :, :], [[1, P], [0, TOPK * NJ]])

            def gather(s, par, ring):
                pool.wait_ge(src_ok, s + 1)
                if ring:
                    pool.wait_ge(tr_done, s - 1)
                pool.sem_inc(pool_go, 1)
                for t in range(TB):
                    pool.indirect_dma_start(
                        out=gathered[:, par, t, :], out_offset=None, in_=h_rows,
                        in_offset=bass.IndirectOffsetOnAxis(ap=src_cur[:, par, t:t + 1], axis=0),
                    ).then_inc(rows_in[par], 16)

            def scatter(s, par, halves=False):
                pool.wait_ge(y_half if halves else y_ok, 1 if halves else s + 1)
                pool.wait_ge(dst_ok, s + 1)
                pool.sem_inc(pool_go, 1)
                for t in range(TB):
                    if halves and t == 1:
                        pool.wait_ge(y_ok, s + 1)
                    pool.indirect_dma_start(
                        out=y_rows, out_offset=bass.IndirectOffsetOnAxis(ap=dst_cur[:, par, t:t + 1], axis=0),
                        in_=y_sb[:, par, t, :], in_offset=None, bounds_check=TOPK * N - 1, oob_is_err=False,
                    ).then_inc(y_out[par], 16)

            def high(s, par, ring):
                for bank in range(BANKS):
                    pool.wait_ge(relu_ok, BANKS * s + bank + 1)
                    if ring and bank == 0:
                        pool.wait_ge(l2_done, s - 1)
                    pool.sem_inc(pool_go, 1)
                    pool.tensor_scalar(hid[:, par, 0, 2 * bank:2 * bank + 2, :], relu[:, bank % 2, :, :],
                                       1.0, 0.0, ALU.mult, ALU.add).then_inc(hid_hi, 1)

            pool.wait_ge(hrows_out, 16 * NJ)
            gather(0, 0, False)
            gather(1, 1, False)
            for s in range(2):
                gather(s + 2, s, True)
                high(s, s, False)
            with pool.Fori(1, LOOP.stop) as m:
                for par in range(2):
                    s = 2 * m + par
                    gather(s + 2, par, True)
                    high(s, par, True)
                    scatter(s - 2, par)
            high(NS - 1, 0, True)
            scatter(NS - 3, 0)
            scatter(NS - 2, 1)
            scatter(NS - 1, 0, halves=True)

            for g in range(NPAIR):
                par = g % 2
                f = FD[par].rearrange("p (i n) -> p i n", i=2)
                if g >= 2:
                    pool.wait_ge(t_mm, g - 1)
                if g > 0:
                    pool.wait_ge(t_f, g + 1)
                    pool.wait_ge(t_keep, g + 1)
                    pool.tensor_tensor(GF[par], GG[par], FV[par], ALU.mult).then_inc(t_gf, 1)
                pool.wait_ge(t_fd, g + 1)
                for dst, by, done in ((U2, grid[:, 2:3, :, :].rearrange("p a q d -> p a (q d)"), t_u2),
                                      (PP, gr[:, 0:1, :], t_p), (PQ, gr[:, 1:2, :], t_q)):
                    if g == NPAIR - 1 and done is t_q:
                        continue
                    pool.tensor_tensor(dst[par].rearrange("p (i n) -> p i n", i=2), by.broadcast_to([P, 2, 512]), f,
                                       ALU.mult).then_inc(done, 1)

        @block.tensor
        def _(pe):
            def style(i):
                if i == 0:
                    pe.wait_ge(sty_in, 32)
                    pe.wait_ge(sty_dve, 1)
                    last = pe.matmul(banks[1][0:SE, 0:NB], emb[:, :], oh_s[:, :], start=True, stop=True)
                else:
                    pe.wait_ge(sty_act, i)
                if i == 1:
                    last = pe.matmul(banks[1][:, 8:8 + NB], hw1[:, :], se_t[:, :], start=True, stop=True)
                elif i == 2:
                    last = pe.matmul(banks[1][:, 16:16 + NB], hw2[:, :], hy1[:, :], start=True, stop=True)
                elif i == 3:
                    last = pe.matmul(banks[1][0:SH // 2, 24:24 + NB], sw1[:, :], hy2[:, :], start=True, stop=True)
                elif i == 4:
                    for c in range(4):
                        last = pe.matmul(banks[1][:, 32 + 8 * c:40 + 8 * c], sw2[:, P * c:P * c + P], sy1[:, :],
                                         start=True, stop=True)
                last.then_inc(sty_pe, 1)

            pe.wait_ge(ident_in, 16)

            def forward(b):
                pe.wait_ge(z_ok, b + 1)
                if b >= 2:
                    pe.wait_ge(pre_ok, b - 1)
                for k in range(KD):
                    for q in range(2):
                        last = pe.transpose(banks[4 + b % 2][:, T * k + P * q:T * k + P * q + P],
                                            z[:, (2 * b + q) % 4, P * k:P * k + P], ident)
                last.then_inc(fwd_t, 1)

            def back(b):
                pe.wait_ge(ht_ok, b + 1)
                if b >= 2:
                    pe.wait_ge(*rows_taken(b - 2))
                for q in range(2):
                    for k in range(KD):
                        at = (P + E) * k
                        last = pe.matmul(banks[(6 if b % 2 == 0 else 2) + q][:, at:at + P + E],
                                         hT[:, k, T * b + P * q:T * b + P * q + P], eye_rw[:, k, :],
                                         start=True, stop=True)
                last.then_inc(back_t, 1)

            for i in range(NB + 3):
                if i < NB:
                    forward(i)
                if i == 0:
                    for n in range(STYLE):
                        style(n)
                if i == 3:
                    pe.wait_ge(eye_ok, 1)
                if i >= 3:
                    back(i - 3)

            pe.wait_ge(m_ok, 1)
            rank = banks[2][:, 0:NJ * E]
            pe.matmul(rank, before_bf[:, :], m_bf[:, :, :].rearrange("p j e -> p (j e)"), start=True, stop=False)
            for d in range(1, NJ):
                pe.matmul(rank[:, E * d:NJ * E], ones_bf[:, :],
                          m_bf[:, 0:NJ - d, :].rearrange("p j e -> p (j e)"), start=False, stop=(d == NJ - 1))
            for j in range(NJ):
                last = pe.matmul(banks[3][:, 0:E], ones_bf[:, :], m_bf[:, j, :], start=(j == 0), stop=(j == NJ - 1))
            last.then_inc(rank_ok, 1)

            pe.wait_ge(tok0_ok, 1)
            pe.wait_ge(tok_ok, 1)
            for t in range(TOPK * NJ):
                if t % CHUNK == 0:
                    pe.wait_ge(ohrow_ok, t // CHUNK + 1)
                for part in range(2):
                    last = pe.matmul(banks[1][:, 128:128 + NC], oh_row[:, :, t], tok[:, part, :, t],
                                     start=(t == 0 and part == 0), stop=(t == TOPK * NJ - 1 and part == 1))
            last.then_inc(perm_mm, 1)

            def turn(s, par, mr, first=False, bank=6):
                pe.wait_ge(rows_in[par], mr)
                if not first:
                    pe.wait_ge(h_hi, s)
                    pe.wait_ge(h_lo, s)
                for k in range(KD):
                    for t in range(TB):
                        last = pe.transpose(banks[bank][:, ST * k + P * t:ST * k + P * t + P],
                                            gathered[:, par, t, P * k:P * k + P], ident)
                last.then_inc(tr_done, 1)

            PARTS = ((0, 0), (0, 1), (1, 0))

            def layer1(s, par, first=False):
                pe.wait_ge(w1_hi, s + 1)
                pe.wait_ge(w1_lo, s + 1)
                pe.wait_ge(h_hi, s + 1)
                pe.wait_ge(h_lo, s + 1)
                for blk in range(FB):
                    bank = blk // 2
                    if blk % 2 == 0 and not first:
                        pe.wait_ge(relu_ok, BANKS * s + bank - 3)
                    n = 0
                    for k in range(KD):
                        for w, h in PARTS:
                            at = (k * FB + blk) * P
                            last = pe.matmul(banks[bank][:, ST * (blk % 2):ST * (blk % 2) + ST],
                                             w_split[:, 0, par, w, at:at + P], slot_h[:, par, h, k, :],
                                             start=(n == 0), stop=(n == 3 * KD - 1))
                            n += 1
                    if blk % 2:
                        last.then_inc(l1_done, 1)

            def layer2(s, par, ring, halves=False):
                pe.wait_ge(w2_hi, s + 1)
                pe.wait_ge(w2_lo, s + 1)
                pe.wait_ge(hid_lo, BANKS * (s + 1))
                if ring:
                    pe.wait_ge(y_ok, s - 1)
                for t in range(TB):
                    bank = 4 + par
                    if halves and t == 1:
                        pe.wait_ge(y_ok, s)
                        bank = 5 - par
                    n = 0
                    for blk in range(FB):
                        for h, w in PARTS:
                            last = pe.matmul(banks[bank][:, D * t:D * t + D],
                                             hid[:, par, h, blk, P * t:P * t + P],
                                             w_split[:, 1, par, w, D * blk:D * blk + D],
                                             start=(n == 0), stop=(n == 3 * FB - 1))
                            n += 1
                    if halves and t == 0:
                        last.then_inc(l2_half, 1)
                last.then_inc(l2_done, 1)

            turn(0, 0, 32, first=True)
            turn(1, 1, 32, first=True, bank=7)
            layer1(0, 0, first=True)
            layer1(1, 1)
            turn(2, 0, 64)
            layer2(0, 0, False)
            layer1(2, 0)
            turn(3, 1, 64)
            layer2(1, 1, False)
            with pe.Fori(1, LOOP.stop) as m:
                layer1(2 * m + 1, 1)
                turn(2 * m + 2, 0, 32 * m + 64)
                layer2(2 * m, 0, True)
                layer1(2 * m + 2, 0)
                turn(2 * m + 3, 1, 32 * m + 64)
                layer2(2 * m + 1, 1, True)
            layer2(NS - 1, 0, True, halves=True)

            def rows_mm(g, q, w, v, k, start=False, stop=False):
                v = v.rearrange("p (i q d) -> p q i d", i=2, q=2)
                return pe.matmul(banks[2 * g + q].rearrange("p (i d) -> p i d", i=2), w, v[:, k, :, :],
                                 start=start, stop=stop)

            def along_rows(g, col, u, start=False):
                for q in range(2):
                    for k in range(2):
                        at = col + T * k + P * q
                        rows_mm(g, q, cst[:, at:at + P], u[g % 2], k, start=start and k == 0)

            for g in range(NPAIR + 1):
                if g >= 1:
                    pe.wait_ge(t_s, g)
                    for q in range(2):
                        last = rows_mm(g - 1, q, ident, SM[(g - 1) % 2], q, stop=True)
                        if g == NPAIR or q == 1:
                            last.then_inc(t_mm, 1)
                if g < NPAIR:
                    if g not in JOINED:
                        pe.wait_ge(*kept(g))
                        for q in range(2):
                            rows_mm(g, q, ident, GF[g % 2], q, start=True)
                    pe.wait_ge(t_u2, g + 1)
                    along_rows(g, C_D2, U2, start=g in JOINED)
                    pe.wait_ge(t_u1, g + 1)
                    along_rows(g, C_D1, U1)

        @block.vector
        def _(dve):
            steps = [0]

            def link(ins):
                steps[0] += 1
                ins.then_inc(chain, 1)
                dve.wait_ge(chain, steps[0])

            def chained(ins):
                steps[0] += 1
                ins.then_inc(chain, 1)

            link(dve.memset(ones8[:, :], 1.0))

            def front(i, tokens=True, channels=True):
                chan, aff = i - 3, i - 4
                do_tok = tokens and i < NB
                do_chan, do_aff = channels and 0 <= chan < NB, channels and 0 <= aff < NB
                if do_tok:
                    if i % 2 == 0:
                        dve.wait_ge(x_in[i // 2], 16)
                    for j in range(2 * i, 2 * i + 2):
                        last = dve.bn_stats(st1[:, j, :], x_sb[:, j, :])
                b = i - 1
                if tokens and 0 <= b < NB:
                    dve.wait_ge(rs1_ok, b + 1)
                    if b >= 2:
                        dve.wait_ge(fwd_t, b - 1)
                    for j in range(2 * b, 2 * b + 2):
                        norm = dve.tensor_scalar(z[:, j % 4, :], x_sb[:, j, :], mv1[:, j, 0:1], rs1[:, j:j + 1],
                                                 ALU.subtract, ALU.mult)
                    norm.then_inc(z_ok, 1)
                if do_aff:
                    dve.wait_ge(rs2_ok, aff + 1)
                    last = dve.tensor_tensor(aff_a[:, aff, :], rs2[:, aff, :], gam[:, :, aff], ALU.mult)
                if do_chan:
                    dve.wait_ge(pre_ok, chan + 1)
                    for k in range(KD):
                        last = dve.bn_stats(st2[:, chan, k, :], h_pre[:, k, T * chan:T * chan + T])
                if not (do_tok or do_aff or do_chan):
                    return
                link(last)
                if do_tok:
                    for j in range(2 * i, 2 * i + 2):
                        last = dve.bn_aggr(mv1[:, j, :], st1[:, j, :])
                if do_aff:
                    last = dve.tensor_tensor(aff_m[:, aff, :], mv2[:, aff, :, 0], aff_a[:, aff, :], ALU.mult)
                if do_chan:
                    for k in range(KD):
                        last = dve.bn_aggr(mv2[:, chan, k, :], st2[:, chan, k, :])
                link(last)
                if do_tok:
                    dve.tensor_scalar(var1[:, 2 * i:2 * i + 2], mv1[:, 2 * i:2 * i + 2, 1], 1e-5, None,
                                      ALU.add).then_inc(var1_ok, 1)
                if do_chan:
                    dve.tensor_scalar(var2[:, chan, :], mv2[:, chan, :, 1], 1e-8, None, ALU.add).then_inc(var2_ok, 1)
                if do_aff:
                    dve.tensor_tensor(aff_b[:, aff, :], sty[:, KD:2 * KD, aff], aff_m[:, aff, :],
                                      ALU.subtract).then_inc(aff_ok, 1)

            def late_rows(b):
                dve.wait_ge(back_t, b + 1)
                at = 6 if b % 2 == 0 else 2
                link(dve.tensor_copy(h_tok[:, 2 * b:2 * b + 2, :, :],
                                     psum[:, at:at + 2, 0:KD * (P + E)].rearrange("p j (k n) -> p j k n", k=KD)))
                dve.sem_inc(htok_late, 1)

            for i in range(NB + 6):
                if i == 2:
                    dve.wait_ge(sty_in, 32)
                    dve.wait_ge(ident_in, 16)
                    link(dve.tensor_copy(id_f[:, :], id_i[:, :]))
                    dve.tensor_scalar(oh_s[:, :], id_f[:, :], cst[0:S_SUB, C_PART:C_PART + 1], None,
                                      ALU.is_equal).then_inc(sty_dve, 1)
                if i == 2:
                    for k in range(KD):
                        dve.tensor_copy(eye_rw[:, k, 0:P], ident)
                    dve.tensor_copy(eye_rw[:, :, P:P + E], rw_sb).then_inc(eye_ok, 1)
                if i == 4:
                    front(i, channels=False)
                    dve.wait_ge(sty_act, 8)
                    link(dve.tensor_scalar(grelu[:, :, :], sty[:, 0:KD, :], 0.0, None, ALU.max))
                    link(dve.tensor_tensor(gsum[:, :, :], grelu[:, :, :], gln[:, :, :], ALU.add))
                    link(dve.tensor_scalar(gam[:, :, :], gsum[:, :, :], 1e-8, None, ALU.add))
                if i == NB:
                    dve.wait_ge(cst_in, 16)
                    dve.memset(ones_bf[:, :], 1.0)
                    dve.tensor_copy(before_bf[:, :], cst[:, C_BEFORE:C_BEFORE + P])
                front(i, tokens=(i != 4))
                if LATE <= i - 6 < NB:
                    late_rows(i - 6)

            dve.wait_ge(htok_ok, LATE)
            link(dve.tensor_tensor(lg[:, :, :], h_tok[:, :, 0, P:P + E], h_tok[:, :, 1, P:P + E], ALU.add))
            expert = cst[:, C_EXPERT:C_EXPERT + NJ * E].rearrange("p (j e) -> p j e", e=E)

            def spread(v):
                return v.rearrange("p (j a) -> p j a", a=1).broadcast_to([P, NJ, E])

            for c, src in enumerate((lg, lg2)):
                link(dve.tensor_reduce(mx[:, c, :], src[:, :, :], AX_X, ALU.max))
                link(dve.tensor_tensor(eq[:, :, :], src[:, :, :], spread(mx[:, c, :]), ALU.is_equal))
                link(dve.scalar_tensor_tensor(out=cand[:, :, :], in0=eq[:, :, :], scalar=-2.0 * E, in1=expert,
                                              op0=ALU.mult, op1=ALU.add))
                link(dve.tensor_reduce(least[:, :], cand[:, :, :], AX_X, ALU.min))
                link(dve.tensor_tensor(oh[:, c, :, :], cand[:, :, :], spread(least[:, :]), ALU.is_equal))
                if c == 0:
                    link(dve.scalar_tensor_tensor(out=lg2[:, :, :], in0=oh[:, 0, :, :], scalar=-3e38,
                                                  in1=lg[:, :, :], op0=ALU.mult, op1=ALU.add))
            dve.tensor_tensor(m_bf[:, :, :], oh[:, 0, :, :], oh[:, 1, :, :], ALU.add).then_inc(m_ok, 1)
            dve.tensor_tensor(gap[:, :], mx[:, 1, :], mx[:, 0, :], ALU.subtract).then_inc(gap_ok, 1)

            dve.wait_ge(e2_ok, 1)
            link(dve.tensor_scalar(den[:, :], e2[:, :], 1.0, None, ALU.add))
            link(dve.reciprocal(gates[:, 0, :], den[:, :]))
            link(dve.tensor_tensor(gates[:, 1, :], e2[:, :], gates[:, 0, :], ALU.mult))

            dve.wait_ge(rank_ok, 1)
            link(dve.tensor_scalar(cnt_i[:, :], banks[3][:, 0:E], float(ST - 1), None, ALU.add))
            link(dve.tensor_scalar(tl_i[:, :], cnt_i[:, :], ST.bit_length() - 1, None, ALU.arith_shift_right))
            link(dve.tensor_copy(tl_f[:, :], tl_i[:, :]))
            link(dve.tensor_tensor_scan(t_end[:, :], ones8[:, :], tl_f[:, :], 0.0, ALU.mult, ALU.add))
            link(dve.tensor_tensor(t_off[:, :], t_end[:, :], tl_f[:, :], ALU.subtract))
            chained(dve.tensor_tensor(e_cmp[:, :, :],
                                      t_off[0:1, :].rearrange("p (a e) -> p a e", a=1).broadcast_to([1, NS, E]),
                                      cst[0:1, C_SLOT:C_SLOT + NS * E].rearrange("p (s e) -> p s e", e=E), ALU.is_le))
            link(dve.tensor_scalar(base[:, :], t_off[:, :], float(ST), None, ALU.mult))
            chained(dve.tensor_reduce(e_sum[:, :], e_cmp[:, :, :], AX_X, ALU.add))
            link(dve.tensor_tensor(pos[:, :, :], banks[2][:, 0:NJ * E].rearrange("p (j e) -> p j e", e=E),
                                   base[:, :].rearrange("p (a e) -> p a e", a=1).broadcast_to([P, NJ, E]), ALU.add))
            dve.tensor_scalar(e_idx[:, :], e_sum[:, :], -1.0, None, ALU.add).then_inc(e_ok, 1)
            link(dve.tensor_tensor(
                pick[:, :, :, :].rearrange("p c j e -> p c (j e)"), oh[:, :, :, :].rearrange("p c j e -> p c (j e)"),
                pos[:, :, :].rearrange("p (a j) e -> p a (j e)", a=1).broadcast_to([P, TOPK, NJ * E]), ALU.mult))
            link(dve.tensor_reduce(slot_f[:, :], pick[:, :, :, :].rearrange("p c j e -> p (c j) e"), AX_X, ALU.add))
            link(dve.tensor_copy(slot_i[:, :], slot_f[:, :]))
            dve.tensor_scalar(col_i[:, :], slot_i[:, :], P.bit_length() - 1, None, ALU.arith_shift_right)
            link(dve.tensor_scalar(low_i[:, :], slot_i[:, :], P - 1, None, ALU.bitwise_and))
            dve.tensor_copy(col_f[:, :], col_i[:, :])
            link(dve.tensor_copy(low_f[:, :], low_i[:, :]))
            TC = TOPK * NJ

            def by_tile(v, n):
                return v.rearrange("p (a t) -> p a t", a=1).broadcast_to([P, n, TC])

            dve.wait_ge(iota_ok, 3)
            dve.tensor_tensor(oh_col[:, :, :], by_tile(col_f[:, :], NC), col_of[:, :, :],
                              ALU.is_equal).then_inc(ohcol_ok, 1)
            dve.wait_ge(ohcol_ok, 1)
            dve.tensor_tensor(tok[:, 1, :, :], oh_col[:, :, :], by_tile(tile_of[:, :], NC),
                              ALU.mult).then_inc(tok_ok, 1)
            for n in range(TC // CHUNK):
                at = slice(CHUNK * n, CHUNK * n + CHUNK)
                dve.tensor_tensor(
                    oh_row[:, :, at],
                    low_f[:, at].rearrange("p (a t) -> p a t", a=1).broadcast_to([P, P, CHUNK]), row_of[:, :, at],
                    ALU.is_equal).then_inc(ohrow_ok, 1)
            dve.wait_ge(perm_mm, 1)
            num = banks[1][:, 128:128 + NC]
            link(dve.tensor_scalar(num_i[:, :], num, float(N - 1), None, ALU.add))
            dve.tensor_scalar(src_cur[:, :, :], num_i[:, 0:2 * TB].rearrange("p (s t) -> p s t", t=TB), N - 1, None,
                              ALU.bitwise_and).then_inc(src_ok, 2)
            dve.tensor_scalar(src_i[:, 0:NC], num_i[:, :], N - 1, None, ALU.bitwise_and)
            dve.memset(src_i[:, NC:NC + TB], 0)
            link(dve.tensor_scalar(num_f[:, :], num, 0.0, EMPTY, ALU.is_equal, ALU.mult))
            link(dve.scalar_tensor_tensor(out=dst_i[:, :], in0=num, scalar=-1.0, in1=num_f[:, :],
                                          op0=ALU.add, op1=ALU.add))

            def source(s, par, ring):
                dve.wait_ge(rows_in[par], ring)
                dve.tensor_copy(src_cur[:, par, :], src_i[:, bass.DynSlice(TB * s, TB)]).then_inc(src_ok, 1)

            def low_w1(s, par):
                dve.wait_ge(w1_hi, s + 1)
                dve.tensor_tensor(w_split[:, 0, par, 1, :].rearrange("p (k b f) -> p (k b) f", k=KD, b=FB)
                                  .rearrange("p (k b) f -> p k b f", k=KD),
                                  w1_raw[par].rearrange("p (k f b) -> p k b f", k=KD, b=FB),
                                  w_split[:, 0, par, 0, :].rearrange("p (k b f) -> p k b f", k=KD, b=FB).bitcast(F32),
                                  ALU.subtract).then_inc(w1_lo, 1)

            def low_w2(s, par):
                dve.wait_ge(w2_hi, s + 1)
                dve.tensor_tensor(w_split[:, 1, par, 1, :], w2_raw[par], w_split[:, 1, par, 0, :].bitcast(F32),
                                  ALU.subtract).then_inc(w2_lo, 1)

            def low_h(s, par, bank=6):
                dve.wait_ge(h_hi, s + 1)
                dve.tensor_tensor(slot_h[:, par, 1, :, :], banks[bank].rearrange("p (k n) -> p k n", k=KD),
                                  slot_h[:, par, 0, :, :].bitcast(F32), ALU.subtract).then_inc(h_lo, 1)

            def low_hid(s, par):
                for bank in range(BANKS):
                    dve.wait_ge(hid_hi, BANKS * s + bank + 1)
                    dve.tensor_tensor(hid[:, par, 1, 2 * bank:2 * bank + 2, :], relu[:, bank % 2, :, :],
                                      hid[:, par, 0, 2 * bank:2 * bank + 2, :].bitcast(F32),
                                      ALU.subtract).then_inc(hid_lo, 1)

            def finish(s, par, ring, halves=False):
                e = dve.value_load(e_idx[0:1, bass.DynSlice(s, 1)], min_val=0, max_val=E - 1)
                if ring is not None:
                    dve.wait_ge(y_out[par], ring)
                dve.tensor_copy(dst_cur[:, par, :], dst_i[:, bass.DynSlice(TB * s, TB)]).then_inc(dst_ok, 1)
                y = banks[4 + par].rearrange("p (t d) -> p t d", t=TB)
                if halves:
                    dve.wait_ge(l2_half, 1)
                    dve.tensor_tensor(y_sb[:, par, 0:1, :], y[:, 0:1, :], b2_all[:, bass.DynSlice(e, 1), :],
                                      ALU.add).then_inc(y_half, 1)
                    y, t0 = banks[5 - par].rearrange("p (t d) -> p t d", t=TB)[:, 1:TB, :], 1
                else:
                    t0 = 0
                dve.wait_ge(l2_done, s + 1)
                dve.tensor_tensor(y_sb[:, par, t0:TB, :], y,
                                  b2_all[:, bass.DynSlice(e, 1), :].broadcast_to([P, TB - t0, D]),
                                  ALU.add).then_inc(y_ok, 1)

            low_w1(0, 0)
            low_h(0, 0)
            low_w1(1, 1)
            low_h(1, 1, bank=7)
            dve.wait_ge(exp_in, 32)

            def dve_step(s, par, gathered_by, scattered_by, first=False, turned=False):
                source(s + 2, par, gathered_by)
                if not first:
                    finish(s - 2, par, scattered_by)
                if turned:
                    low_w2(s, par)
                    low_hid(s, par)
                else:
                    low_w1(s + 1, 1 - par)
                    low_hid(s, par)
                    low_h(s + 1, 1 - par)
                    low_w2(s, par)

            for s in range(4):
                dve_step(s, s % 2, 32 * (s // 2) + 32, None, first=s < 2, turned=s == 0)
            with dve.Fori(2, LOOP.stop) as m:
                for par in range(2):
                    dve_step(2 * m + par, par, 32 * m + 32, 32 * m - 32)
            dve.wait_ge(grid_in, 64)
            A0, A1, B0, B1, B2 = (grid[:, n, :, :].rearrange("p q d -> p (q d)") for n in range(5))
            dve.tensor_scalar(dt_n[:, :], dt_b[:, :], -1.0, None, ALU.mult)
            dve.tensor_tensor(gr[:, 0, :], B1, A1, ALU.subtract)
            dve.tensor_tensor(gr[:, 1, :], B1, A1, ALU.add)
            ew = cst[:, C_EDGE:C_EDGE + 24].rearrange("p (n c) -> p n c", n=3)
            for at, cols in ((slice(0, 4), slice(0, 4)), (slice(4, 8), slice(D - 4, D))):
                for n, gi, dst in ((0, 3, edge_w[:, 0, 0:KD, at]), (1, 1, edge_t[:, :, at]),
                                   (2, 4, edge_w[:, 1, 0:KD, at])):
                    last = dve.tensor_tensor(dst, grid[:, gi, :, cols], ew[:, n:n + 1, at].broadcast_to([P, KD, 4]),
                                             ALU.mult)
            link(last)
            link(dve.tensor_tensor(edge_w[:, 0, 0:KD, :], edge_w[:, 0, 0:KD, :], edge_t[:, :, :], ALU.add))
            dve.tensor_copy(edge_w[:, :, KD:2 * KD, :], edge_w[:, :, 0:KD, :])
            dve.tensor_scalar(gr[:, 2, :], B2, 0.5, None, ALU.mult)
            dve.tensor_scalar(gr[:, 0:2, :], gr[:, 0:2, :], 0.5, None, ALU.mult).then_inc(grids_ok, 1)

            last_round = (NS - 1) // 2
            finish(NS - 3, 0, 32 * (last_round - 1))
            low_hid(NS - 1, 0)
            low_w2(NS - 1, 0)
            finish(NS - 2, 1, 32 * (last_round - 1))
            finish(NS - 1, 0, 32 * last_round, halves=True)

            dve.wait_ge(grids_ok, 1)

            def edge_cols(v):
                ends = v.rearrange("p r (s c) -> p r s c", c=4)
                return ends[:, :, 0:D // 4:D // 4 - 1, :]

            def add_up(g):
                if g >= 2:
                    dve.wait_ge(t_fd, g - 1)
                    if g > 2:
                        dve.wait_ge(*kept(g - 2))
                if g > 0:
                    dve.wait_ge(t_gated, 2 * g - 1)
                    link(dve.tensor_tensor(F0[g % 2], Y1[g % 2],
                                           x_sb[:, 4 * g:4 * g + 4, :].rearrange("p j d -> p (j d)"), ALU.add))
                    dve.wait_ge(t_gated, 2 * g)
                    last = dve.tensor_tensor(FV[g % 2], Y2[g % 2], F0[g % 2], ALU.add)
                else:
                    for i in range(2):
                        for c, y, dst in ((0, Y1, F0), (1, Y2, FV)):
                            dve.wait_ge(y_first[c][i], 16)
                            for j in range(2 * i, 2 * i + 2):
                                at = slice(D * j, D * j + D)
                                last = dve.scalar_tensor_tensor(
                                    out=dst[0][:, at], in0=y[0][:, at], scalar=gates[:, c, j:j + 1],
                                    in1=x_sb[:, j, :] if c == 0 else F0[0][:, at], op0=ALU.mult, op1=ALU.add)
                            if c == 0:
                                link(last)
                        if i == 0:
                            last.then_inc(t_first, 1)
                last.then_inc(t_f, 1)
                dve.wait_ge(t_f, g + 1)

            def wide(v):
                return v.rearrange("p (i n) -> p i n", i=2)

            def over(v):
                return v.rearrange("p (a n) -> p a n", a=1).broadcast_to([P, 2, 512])

            def rows_of(v):
                return v.rearrange("p (r d) -> p r d", d=D)

            def products(g):
                par = g % 2
                f, a, b, u1 = FD[par], PA[par], PB[par], U1[par]
                if g >= 2:
                    dve.wait_ge(t_mm, g - 1)
                if g == 0:
                    dve.wait_ge(t_keep, 1)
                    dve.tensor_tensor(GF[par], GG[par], FV[par], ALU.mult).then_inc(t_gf0, 1)
                dve.wait_ge(t_fd, g + 1)
                dve.tensor_tensor(wide(a), over(A0), wide(f), ALU.mult)
                dve.tensor_tensor(wide(b), over(gr[:, 2, :]), wide(f), ALU.mult)
                for kind in range(2):
                    last = dve.tensor_tensor(edge_p[:, par, kind, :, :, :], edge_cols(rows_of(f)),
                                             edge_w[:, kind, :, :].rearrange("p r (s c) -> p r s c", s=2), ALU.mult)
                link(last)
                bv, cv = rows_of(b), rows_of(CC[par])
                dve.tensor_reduce(cv[:, :, 0:D:D - 1], edge_p[:, par, 1, :, :, :], AX_X, ALU.add)
                dve.tensor_reduce(rows_of(SM[par])[:, :, 0:D:D - 1], edge_p[:, par, 0, :, :, :], AX_X, ALU.add)
                link(dve.tensor_tensor(cv[:, :, 1:D - 1], bv[:, :, 2:D], bv[:, :, 0:D - 2], ALU.subtract))
                dve.tensor_tensor(u1, CC[par], a, ALU.subtract).then_inc(t_u1, 1)

            def along_columns(g):
                par = g % 2
                pv, qv = rows_of(PP[par]), rows_of(PQ[par])
                if g == NPAIR - 1:
                    link(dve.tensor_tensor(wide(PQ[par]), over(gr[:, 1, :]), wide(FD[par]), ALU.mult))
                else:
                    dve.wait_ge(t_q, g + 1)
                dve.wait_ge(t_p, g + 1)
                last = dve.tensor_tensor(rows_of(SM[par])[:, :, 1:D - 1], pv[:, :, 2:D], qv[:, :, 0:D - 2], ALU.add)
                if g in JOINED:
                    link(last)
                    dve.wait_ge(*kept(g))
                    last = dve.tensor_tensor(SM[par], SM[par], GF[par], ALU.add)
                last.then_inc(t_s, 1)

            for g in range(NPAIR + 1):
                if g < NPAIR:
                    add_up(g)
                if g >= 1:
                    along_columns(g - 1)
                if g < NPAIR:
                    products(g)


_INS = ['x', 'itok_B_6_14', 'condB_dt', 'L0_cond_exp_w1', 'L0_cond_exp_b1', 'L0_cond_exp_w2', 'L0_cond_exp_b2',
        'L1_cond_A_grid', 'L1_cond_B_grid']


def kernel(**inputs):
    import concourse.bacc as _bacc
    from concourse.bass_utils import run_bass_kernel_spmd as _run

    nc = _bacc.Bacc("TRN2", target_bir_lowering=False, num_devices=1)
    arrays, args = {}, []
    given = {name: np.ascontiguousarray(inputs[name]) for name in _INS}
    for name, a in {**given, "small": pack(inputs), "constants": constants()}.items():
        arrays[f"in_{name}_dram"] = a
        args.append(nc.dram_tensor(f"in_{name}_dram", a.shape, mybir.dt.from_np(a.dtype), kind="ExternalInput").ap())
    args.append(nc.dram_tensor("out_0_dram", (NB, T, D), F32, kind="ExternalOutput").ap())
    moe_then_stencil(nc, *args)
    r = _run(nc, [arrays], core_ids=[0])
    return r.results[0]["out_0_dram"]
```
